# Optimizing a Trainium2 kernel written in Bass

```python
import numpy as np
import jax
import jax.numpy as jnp

def _softmax(x, axis=-1):
    return jax.nn.softmax(x, axis=axis)

def _gelu(x):
    return jax.nn.gelu(x, approximate=True)

def _silu(x):
    return jax.nn.silu(x)

def _sigmoid(x):
    return jax.nn.sigmoid(x)

def _layernorm(x, axis=-1, eps=1e-05):
    m = jnp.mean(x, axis=axis, keepdims=True)
    v = jnp.var(x, axis=axis, keepdims=True)
    return (x - m) / jnp.sqrt(v + eps)

def _scatter_add(tgt, idx, src, axis=0):
    return tgt.at[idx].add(src)

def _segment_sum(src, seg, n):
    return jax.ops.segment_sum(src, seg, n)
kernel_name = 'mk_seq_preln_d1_jaxref_r4_a8ec77'

def setup_inputs(seed: int=0):
    np.random.seed(seed)
    _w = jnp.asarray

    def _L0_attn_setup():
        import jax, jax.numpy as jnp
        import numpy as np
        HEADS = 8
        SPARSITY = 0.5
        key = jax.random.key(seed)
        ks = jax.random.split(key, 6)
        B, N, D = (16, 256, 256)
        s = 1.0 / np.sqrt(D)
        return {'x': jax.random.normal(ks[0], (B, N, D), jnp.float32), 'Wq': jax.random.normal(ks[1], (D, D), jnp.float32) * s, 'bq': jnp.zeros((D,), jnp.float32), 'Wk': jax.random.normal(ks[2], (D, D), jnp.float32) * s, 'bk': jnp.zeros((D,), jnp.float32), 'Wv': jax.random.normal(ks[3], (D, D), jnp.float32) * s, 'bv': jnp.zeros((D,), jnp.float32), 'Wo': jax.random.normal(ks[4], (D, D), jnp.float32) * s, 'bo': jnp.zeros((D,), jnp.float32)}
    _L0_attn_in = _L0_attn_setup()

    def _L0_ffn_setup():
        import jax, jax.numpy as jnp
        import numpy as np
        DIM = 256

        def _reference_tuple_inner(x, W_r, W_k, W_v, mu_r, mu_k):
            B, T, C = x.shape
            x_prev = jnp.concatenate([jnp.zeros((B, 1, C), x.dtype), x[:, :-1, :]], axis=1)
            xr = mu_r * x + (1.0 - mu_r) * x_prev
            xk = mu_k * x + (1.0 - mu_k) * x_prev
            r = jax.nn.sigmoid(jnp.einsum('btc,dc->btd', xr, W_r))
            k = jnp.einsum('btc,dc->btd', xk, W_k)
            k_act = jnp.square(jax.nn.relu(k))
            out = r * jnp.einsum('btc,dc->btd', k_act, W_v)
            new_state = x[:, -1, :]
            return (out, new_state)
        key = jax.random.key(seed)
        ks = jax.random.split(key, 6)
        B, T, C = (8, 512, DIM)
        x = jax.random.normal(ks[0], (B, T, C), dtype=jnp.float32)
        s = 1.0 / np.sqrt(C)
        W_r = jax.random.uniform(ks[1], (C, C), jnp.float32, -s, s)
        W_k = jax.random.uniform(ks[2], (C, C), jnp.float32, -s, s)
        W_v = jax.random.uniform(ks[3], (C, C), jnp.float32, -s, s)
        mu_r = jax.random.uniform(ks[4], (C,), jnp.float32)
        mu_k = jax.random.uniform(ks[5], (C,), jnp.float32)
        return {'x': x, 'W_r': W_r, 'W_k': W_k, 'W_v': W_v, 'mu_r': mu_r, 'mu_k': mu_k}
    _L0_ffn_in = _L0_ffn_setup()
    _d = {'L0_attn_x': _L0_attn_in['x'], 'L0_attn_Wq': _L0_attn_in['Wq'], 'L0_attn_bq': _L0_attn_in['bq'], 'L0_attn_Wk': _L0_attn_in['Wk'], 'L0_attn_bk': _L0_attn_in['bk'], 'L0_attn_Wv': _L0_attn_in['Wv'], 'L0_attn_bv': _L0_attn_in['bv'], 'L0_attn_Wo': _L0_attn_in['Wo'], 'L0_attn_bo': _L0_attn_in['bo'], 'L0_ffn_W_r': _L0_ffn_in['W_r'], 'L0_ffn_W_k': _L0_ffn_in['W_k'], 'L0_ffn_W_v': _L0_ffn_in['W_v'], 'L0_ffn_mu_r': _L0_ffn_in['mu_r'], 'L0_ffn_mu_k': _L0_ffn_in['mu_k']}
    _x0 = _d['L0_attn_x']
    _d['L0_attn_x'] = jax.random.normal(jax.random.fold_in(jax.random.key(seed), 1), (16, 1024, 256), dtype=_x0.dtype)
    del _x0
    return _d

def reference(L0_attn_x, L0_attn_Wq, L0_attn_bq, L0_attn_Wk, L0_attn_bk, L0_attn_Wv, L0_attn_bv, L0_attn_Wo, L0_attn_bo, L0_ffn_W_r, L0_ffn_W_k, L0_ffn_W_v, L0_ffn_mu_r, L0_ffn_mu_k):

    def _L0_attn_ref(x, Wq, bq, Wk, bk, Wv, bv, Wo, bo):
        import jax, jax.numpy as jnp
        import numpy as np
        HEADS = 8
        SPARSITY = 0.5
        B, N, D = x.shape
        H = HEADS
        hd = D // H

        def split_heads(t):
            return t.reshape(B, N, H, hd).transpose(0, 2, 1, 3)
        q = split_heads(x @ Wq + bq)
        k = split_heads(x @ Wk + bk)
        v = split_heads(x @ Wv + bv)
        scores = jnp.einsum('bhnd,bhmd->bhnm', q, k) / jnp.sqrt(jnp.float32(hd))
        k_value = max(1, int(N * SPARSITY))
        topk_vals = jax.lax.top_k(scores, k_value)[0]
        threshold = topk_vals[..., -1:]
        scores = jnp.where(scores < threshold, jnp.float32(-1000000000.0), scores)
        attn = jax.nn.softmax(scores, axis=-1)
        out = jnp.einsum('bhnm,bhmd->bhnd', attn, v)
        out = out.transpose(0, 2, 1, 3).reshape(B, N, D)
        return out @ Wo + bo

    def _L0_ffn_ref(x, W_r, W_k, W_v, mu_r, mu_k):
        import jax, jax.numpy as jnp
        import numpy as np
        DIM = 256

        def _reference_tuple_inner(x, W_r, W_k, W_v, mu_r, mu_k):
            B, T, C = x.shape
            x_prev = jnp.concatenate([jnp.zeros((B, 1, C), x.dtype), x[:, :-1, :]], axis=1)
            xr = mu_r * x + (1.0 - mu_r) * x_prev
            xk = mu_k * x + (1.0 - mu_k) * x_prev
            r = jax.nn.sigmoid(jnp.einsum('btc,dc->btd', xr, W_r))
            k = jnp.einsum('btc,dc->btd', xk, W_k)
            k_act = jnp.square(jax.nn.relu(k))
            out = r * jnp.einsum('btc,dc->btd', k_act, W_v)
            new_state = x[:, -1, :]
            return (out, new_state)
        return _reference_tuple_inner(x, W_r, W_k, W_v, mu_r, mu_k)[0]
    x = L0_attn_x
    x = x + _L0_attn_ref(_layernorm(x, axis=-1), L0_attn_Wq, L0_attn_bq, L0_attn_Wk, L0_attn_bk, L0_attn_Wv, L0_attn_bv, L0_attn_Wo, L0_attn_bo)
    x = x + _L0_ffn_ref(_layernorm(x, axis=-1), L0_ffn_W_r, L0_ffn_W_k, L0_ffn_W_v, L0_ffn_mu_r, L0_ffn_mu_k)
    return x

_drawn_inputs = setup_inputs


def setup_inputs(seed=0):
    import zlib

    import numpy as np

    out = dict(_drawn_inputs(seed))
    spreads = {'L0_attn_bq': (0.0, 0.776),
     'L0_attn_bk': (0.0, 0.8),
     'L0_attn_bv': (0.0, 0.1),
     'L0_attn_bo': (0.0, 0.1)}
    factors = {'L0_ffn_W_r': 3.134, 'L0_ffn_mu_r': 6.395}
    for name, (base, spread) in spreads.items():
        noise = np.random.default_rng([zlib.crc32(name.encode()), seed]).standard_normal(out[name].shape)
        drawn = base * np.exp(spread * noise) if base else spread * noise
        out[name] = jnp.asarray(drawn.astype(out[name].dtype))
    for name, factor in factors.items():
        out[name] = (out[name] * factor).astype(out[name].dtype)
    return out
```

```python
import concourse.bass as bass
from concourse import mybir
from contextlib import ExitStack

F32 = mybir.dt.float32
BF16 = mybir.dt.bfloat16
I32 = mybir.dt.int32
ALU = mybir.AluOpType
ACT = mybir.ActivationFunctionType
AX_X = mybir.AxisListType.X

P = 128
B, N, D = 16, 1024, 256
H, HD = 8, 32
KEEP = N // 2
T = N // P
CH = D // P
GH = P // HD
GROUPS = B * H
HALF = N // 2
NB = N // HALF
PARTS = 3
VW = HD + 1
VROW = T * VW + T
EPS = 1e-5
SCALE = float(HD) ** -0.5
RIDGE = 4e-6
SPACING = 0.5 * (2.0 * 3.141592653589793) ** 0.5 / N
REACH = 7
WINDOW = REACH ** 2 + 0.5
TINY = 2.0 ** -21
BELOW = 1.0 - 2.0 ** -24
FAR = 1e20
MARGIN = 2.0 ** -10
ROUNDS = 2
MASKED = (2, 3, 4, 6)
BY_MASK = len(MASKED)


def constants(nc, ctx, block_name_prefix=""):
    ident = ctx.enter_context(nc.sbuf_tensor("ident", [P, P], F32))
    return ident


def wait(engine, semaphore, value):
    if not isinstance(value, int) or value > 0:
        engine.wait_ge(semaphore, value)


def over_batches(engine, batch):
    batch(0)
    with engine.Fori(1, B) as b:
        batch(b)


def make_identity(pool, nc, ident, made):
    nc.gpsimd.memset(ident[:, :], 1.0)
    pool.drain()
    nc.gpsimd.affine_select(out=ident[:, :], in_=ident[:, :], compare_op=ALU.is_equal, fill=0.0, base=0,
                            pattern=[[-1, P]], channel_multiplier=1).then_inc(made, 1)


def project(nc, x, Wq, bq, Wk, bk, Wv, bv, qs, ks, vs):
    ctx = ExitStack()
    with ctx:
        def sb(name, shape, dt=F32):
            return ctx.enter_context(nc.sbuf_tensor(name, shape, dt))

        def sem(name):
            return ctx.enter_context(nc.semaphore(name))

        ident = sb("p_ident", [P, P])
        spread_mask = sb("p_spread_mask", [P, P])
        head_ones = sb("p_head_ones", [P, GH])
        wq = sb("p_wq", [P, CH, D])
        wk = sb("p_wk", [P, CH, D])
        wv = sb("p_wv", [P, CH, D])
        bq_col = sb("p_bq", [P, CH])
        bk_col = sb("p_bk", [P, CH])
        bv_row = sb("p_bv", [P, D])
        exps = sb("p_exps", [P, 2, T * H])
        xt = sb("p_x", [P, T, D])
        bst = sb("p_bst", [P, T, 6])
        mv = sb("p_mv", [P, T, 2])
        var_eps = sb("p_var", [P, T])
        rstd = sb("p_rstd", [P, T])
        xn = sb("p_xn", [P, T, D])
        xT = sb("p_xT", [P, CH, N])
        qT = sb("p_qT", [P, CH, N])
        kT = sb("p_kT", [P, CH, N])
        ksum = sb("p_ksum", [P, CH, NB])
        kmean = sb("p_kmean", [P, CH])
        qrest = sb("p_qrest", [P, CH, N])
        krest = sb("p_krest", [P, CH, N])
        qp = sb("p_qp", [P, PARTS, CH, N], BF16)
        kp = sb("p_kp", [P, PARTS, CH, N], BF16)
        knat = sb("p_knat", [P, T, D])
        cm = sb("p_cm", [P, CH, P])
        prod = sb("p_prod", [P, CH, N])
        sq = sb("p_sq", [P, H, T])
        va = sb("p_va", [P, H, VROW])
        v_view = va[:, :, 0:T * VW].rearrange("p h (t w) -> p h t w", w=VW)
        shift_view = va[:, :, T * VW:VROW]

        tp = [ctx.enter_context(nc.psum_tensor(f"p_tp{i}", [P, HALF], F32)) for i in range(2)]
        pj = [ctx.enter_context(nc.psum_tensor(f"p_pj{i}", [P, HALF], F32)) for i in range(4)]
        ps_c = ctx.enter_context(nc.psum_tensor("p_ps_c", [P, CH, P], F32))
        ps_s = ctx.enter_context(nc.psum_tensor("p_ps_s", [P, T, H], F32))

        weights = sem("p_weights")
        made = sem("p_made")
        x_loaded = sem("p_x_loaded")
        stats = sem("p_stats")
        rstd_ready = sem("p_rstd_ready")
        xn_ready = sem("p_xn_ready")
        tp_done = sem("p_tp_done")
        tp_taken = sem("p_tp_taken")
        pj_done = sem("p_pj_done")
        q_taken = sem("p_q_taken")
        k_taken = sem("p_k_taken")
        v_taken = sem("p_v_taken")
        w_taken = sem("p_w_taken")
        k_centred = sem("p_k_centred")
        q_high = sem("p_q_high")
        q_rest = sem("p_q_rest")
        q_mid = sem("p_q_mid")
        q_low = sem("p_q_low")
        k_high = sem("p_k_high")
        k_rest = sem("p_k_rest")
        k_mid = sem("p_k_mid")
        k_low = sem("p_k_low")
        c_done = sem("p_c_done")
        c_taken = sem("p_c_taken")
        s_done = sem("p_s_done")
        s_taken = sem("p_s_taken")
        shift_ready = sem("p_shift_ready")
        q_stored = sem("p_q_stored")
        k_stored = sem("p_k_stored")
        v_stored = sem("p_v_stored")

        LOADS = 6
        MADE = 3
        block = ctx.enter_context(nc.Block())

        @block.sync
        def _(sp):
            for w, src in ((wq, Wq), (wk, Wk), (wv, Wv)):
                sp.dma_start(w[:, :, :], src.rearrange("(k p) d -> p k d", p=P)).then_inc(weights, 16)
            sp.dma_start(bq_col[:, :], bq.rearrange("(k p) -> p k", p=P),
                             allow_slow_non_contiguous=True).then_inc(weights, 16)
            sp.dma_start(bk_col[:, :], bk.rearrange("(k p) -> p k", p=P),
                             allow_slow_non_contiguous=True).then_inc(weights, 16)
            sp.dma_start(bv_row[:, :], bv.partition_broadcast(P)).then_inc(weights, 16)
            sp.dma_start(xt[:, :, :], x[0].rearrange("(t p) d -> p t d", p=P)).then_inc(x_loaded, 16)

            def store(b):
                sp.wait_ge(q_low, b + 1)
                sp.wait_ge(q_mid, b + 1)
                for c in range(CH):
                    for i in range(PARTS):
                        sp.dma_start(qs[b, c, :, i, :, :], qp[:, i, c, :]).then_inc(q_stored, 16)
                sp.wait_ge(k_low, b + 1)
                sp.wait_ge(k_mid, b + 1)
                for c in range(CH):
                    for i in range(PARTS):
                        sp.dma_start(ks[b, c, :, i, :, :], kp[:, i, c, :]).then_inc(k_stored, 16)
                sp.wait_ge(shift_ready, b + 1)
                sp.wait_ge(v_taken, 4 * b + 4)
                sp.dma_start(vs[b].rearrange("h p w -> p h w"), va[:, :, :]).then_inc(v_stored, 16)

            with sp.Fori(1, B) as b:
                wait(sp, xn_ready, b)
                sp.dma_start(xt[:, :, :], x[b].rearrange("(t p) d -> p t d", p=P)).then_inc(x_loaded, 16)
                store(b - 1)
            store(B - 1)
            sp.wait_ge(q_stored, 16 * CH * PARTS * B)
            sp.wait_ge(k_stored, 16 * CH * PARTS * B)
            sp.wait_ge(v_stored, 16 * B)

        @block.gpsimd
        def _(pool):
            make_identity(pool, nc, ident, made)
            nc.gpsimd.memset(exps[:, 0, :], -0.5)
            nc.gpsimd.memset(exps[:, 1, :], 0.5)
            nc.gpsimd.memset(v_view[:, :, :, HD:VW], 1.0)
            nc.gpsimd.memset(head_ones[:, :], 0.0)
            pool.wait_ge(made, 1)
            nc.gpsimd.tensor_scalar(spread_mask[:, :], ident[:, :], RIDGE / N, None, ALU.mult)
            pool.drain()
            for i in range(GH):
                s = slice(i * HD, (i + 1) * HD)
                nc.gpsimd.memset(head_ones[s, i:i + 1], 1.0)
                nc.gpsimd.tensor_scalar(spread_mask[s, s], spread_mask[s, s], 1.0 / N, None, ALU.add)
            pool.drain().then_inc(made, 1)

            def batch(b):
                pool.wait_ge(stats, b + 1)
                nc.gpsimd.tensor_tensor(rstd[:, :], var_eps[:, :], exps[:, 0, 0:T], ALU.pow).then_inc(rstd_ready, 1)
                pool.wait_ge(q_high, b + 1)
                nc.gpsimd.tensor_tensor(qrest[:, :, :], qT[:, :, :], qp[:, 0, :, :], ALU.subtract).then_inc(q_rest, 1)
                pool.wait_ge(q_mid, b + 1)
                nc.gpsimd.tensor_tensor(qp[:, 2, :, :], qrest[:, :, :], qp[:, 1, :, :], ALU.subtract).then_inc(q_low, 1)
                pool.wait_ge(s_taken, b + 1)
                nc.gpsimd.tensor_tensor(shift_view, sq[:, :, :], exps[:, 1, :].rearrange("p (h t) -> p h t", h=H),
                                        ALU.pow).then_inc(shift_ready, 1)

            over_batches(pool, batch)

        @block.vector
        def _(dve):
            dve.wait_ge(weights, 16 * LOADS)
            dve.wait_ge(made, 2)
            def batch(b):
                dve.wait_ge(x_loaded, 16 * b + 16)
                for t in range(T):
                    nc.vector.bn_stats(bst[:, t, :], xt[:, t, :])
                dve.drain()
                for t in range(T):
                    nc.vector.bn_aggr(mv[:, t, :], bst[:, t, :])
                dve.drain()
                nc.vector.tensor_scalar(var_eps[:, :], mv[:, :, 1], EPS, None, ALU.add).then_inc(stats, 1)
                dve.wait_ge(rstd_ready, b + 1)
                for t in range(T):
                    last = nc.vector.tensor_scalar(xn[:, t, :], xt[:, t, :], mv[:, t, 0:1], rstd[:, t:t + 1],
                                                   ALU.subtract, ALU.mult)
                last.then_inc(xn_ready, 1)
                for g in range(CH):
                    for nh in range(NB):
                        u = 4 + g * NB + nh
                        dve.wait_ge(pj_done, 16 * b + u + 1)
                        nc.vector.tensor_scalar(kT[:, g, nh * HALF:(nh + 1) * HALF], pj[u % 4][:, :],
                                                bk_col[:, g:g + 1], 0.0, ALU.add, ALU.add,
                                                accum_out=ksum[:, g, nh:nh + 1]).then_inc(k_taken, 1)
                dve.drain()
                nc.vector.tensor_tensor(kmean[:, :], ksum[:, :, 0], ksum[:, :, 1], ALU.add)
                dve.drain()
                nc.vector.tensor_scalar(kmean[:, :], kmean[:, :], 1.0 / N, None, ALU.mult)
                dve.drain()
                for g in range(CH):
                    last = nc.vector.tensor_scalar(kT[:, g, :], kT[:, g, :], kmean[:, g:g + 1], None, ALU.subtract)
                last.then_inc(k_centred, 1)
                wait(dve, v_stored, 16 * b)
                for i in range(4):
                    u = 8 + i
                    dve.wait_ge(pj_done, 16 * b + u + 1)
                    for t2 in range(2):
                        last = nc.vector.tensor_tensor(
                            v_view[:, :, 2 * i + t2, 0:HD],
                            pj[u % 4][:, t2 * D:(t2 + 1) * D].rearrange("p (h d) -> p h d", h=H),
                            bv_row[:, :].rearrange("p (h d) -> p h d", h=H), ALU.add)
                    last.then_inc(v_taken, 1)
                dve.wait_ge(k_high, b + 1)
                nc.vector.tensor_tensor(krest[:, :, :], kT[:, :, :], kp[:, 0, :, :], ALU.subtract).then_inc(k_rest, 1)
                dve.wait_ge(c_done, b + 1)
                for g in range(CH):
                    last = nc.vector.tensor_tensor(cm[:, g, :], ps_c[:, g, :], spread_mask[:, :], ALU.mult)
                last.then_inc(c_taken, 1)
                dve.wait_ge(k_mid, b + 1)
                nc.vector.tensor_tensor(kp[:, 2, :, :], krest[:, :, :], kp[:, 1, :, :], ALU.subtract).then_inc(k_low, 1)
                for g in range(CH):
                    for nh in range(NB):
                        u = 12 + g * NB + nh
                        s = slice(nh * HALF, (nh + 1) * HALF)
                        dve.wait_ge(pj_done, 16 * b + u + 1)
                        nc.vector.tensor_tensor(prod[:, g, s], pj[u % 4][:, :], qT[:, g, s], ALU.mult).then_inc(w_taken, 1)
                dve.wait_ge(s_done, b + 1)
                nc.vector.tensor_scalar(sq[:, :, :], ps_s[:, :, :].rearrange("p t h -> p h t"), 4.0, 0.0,
                                        ALU.mult, ALU.max).then_inc(s_taken, 1)

            over_batches(dve, batch)

        @block.scalar
        def _(act):
            act.wait_ge(weights, 16 * LOADS)
            def batch(b):
                wait(act, pj_done, 16 * b)
                for k in range(CH):
                    for half in range(NB):
                        u = k * NB + half
                        act.wait_ge(tp_done, 8 * b + u + 1)
                        nc.scalar.copy(xT[:, k, half * HALF:(half + 1) * HALF], tp[u % 2][:, :]).then_inc(tp_taken, 1)
                wait(act, q_stored, 16 * CH * PARTS * b)
                wait(act, w_taken, 4 * b)
                for g in range(CH):
                    for nh in range(NB):
                        u = g * NB + nh
                        act.wait_ge(pj_done, 16 * b + u + 1)
                        nc.scalar.activation(qT[:, g, nh * HALF:(nh + 1) * HALF], pj[u % 4][:, :], ACT.Identity,
                                             bias=bq_col[:, g:g + 1]).then_inc(q_taken, 1)
                act.wait_ge(q_taken, 4 * b + 4)
                nc.scalar.copy(qp[:, 0, :, :], qT[:, :, :]).then_inc(q_high, 1)
                act.wait_ge(k_centred, b + 1)
                wait(act, k_stored, 16 * CH * PARTS * b)
                nc.scalar.copy(kp[:, 0, :, :], kT[:, :, :]).then_inc(k_high, 1)
                for k in range(CH):
                    for half in range(NB):
                        u = 4 + k * NB + half
                        act.wait_ge(tp_done, 8 * b + u + 1)
                        nc.scalar.copy(knat[:, half * 4:half * 4 + 4, k * P:(k + 1) * P],
                                       tp[u % 2][:, :].rearrange("p (t d) -> p t d", t=4)).then_inc(tp_taken, 1)
                act.wait_ge(k_rest, b + 1)
                nc.scalar.copy(kp[:, 1, :, :], krest[:, :, :]).then_inc(k_mid, 1)
                act.wait_ge(q_rest, b + 1)
                nc.scalar.copy(qp[:, 1, :, :], qrest[:, :, :]).then_inc(q_mid, 1)

            over_batches(act, batch)

        @block.tensor
        def _(pe):
            pe.wait_ge(weights, 16 * LOADS)
            pe.wait_ge(made, 2)
            def batch(b):
                def transposes(unit0, source):
                    for k in range(CH):
                        for half in range(NB):
                            u = unit0 + k * NB + half
                            if u >= 2:
                                pe.wait_ge(tp_taken, 8 * b + u - 1)
                            else:
                                wait(pe, tp_taken, 8 * b)
                            for i in range(4):
                                last = nc.tensor.transpose(tp[u % 2][:, i * P:(i + 1) * P], source(k, half * 4 + i),
                                                           ident[:, :])
                            last.then_inc(tp_done, 1)

                pe.wait_ge(xn_ready, b + 1)
                transposes(0, lambda k, t: xn[:, t, k * P:(k + 1) * P])
                pe.wait_ge(tp_taken, 8 * b + 4)
                for which, w in ((0, wq), (1, wk)):
                    for g in range(CH):
                        for nh in range(NB):
                            u = 4 * which + g * NB + nh
                            if which == 0:
                                wait(pe, w_taken, 4 * b)
                            else:
                                pe.wait_ge(q_taken, 4 * b + g * NB + nh + 1)
                            for k in range(CH):
                                last = nc.tensor.matmul(pj[u % 4][:, :], w[:, k, g * P:(g + 1) * P],
                                                        xT[:, k, nh * HALF:(nh + 1) * HALF],
                                                        start=(k == 0), stop=(k == CH - 1))
                            last.then_inc(pj_done, 1)
                for i in range(4):
                    u = 8 + i
                    pe.wait_ge(k_taken, 4 * b + i + 1)
                    for t2 in range(2):
                        t = 2 * i + t2
                        for k in range(CH):
                            last = nc.tensor.matmul(pj[u % 4][:, t2 * D:(t2 + 1) * D], xT[:, k, t * P:(t + 1) * P],
                                                    wv[:, k, :], start=(k == 0), stop=(k == CH - 1))
                    last.then_inc(pj_done, 1)
                pe.wait_ge(k_centred, b + 1)
                transposes(4, lambda k, t: kT[:, k, t * P:(t + 1) * P])
                pe.wait_ge(tp_taken, 8 * b + 8)
                wait(pe, c_taken, b)
                for g in range(CH):
                    for t in range(T):
                        last = nc.tensor.matmul(ps_c[:, g, :], knat[:, t, g * P:(g + 1) * P],
                                                knat[:, t, g * P:(g + 1) * P], start=(t == 0), stop=(t == T - 1))
                last.then_inc(c_done, 1)
                pe.wait_ge(c_taken, b + 1)
                for g in range(CH):
                    for nh in range(NB):
                        u = 12 + g * NB + nh
                        pe.wait_ge(v_taken, 4 * b + g * NB + nh + 1)
                        nc.tensor.matmul(pj[u % 4][:, :], cm[:, g, :], qT[:, g, nh * HALF:(nh + 1) * HALF],
                                         start=True, stop=True).then_inc(pj_done, 1)
                pe.wait_ge(w_taken, 4 * b + 4)
                wait(pe, s_taken, b)
                for t in range(T):
                    for g in range(CH):
                        last = nc.tensor.matmul(ps_s[:, t, g * GH:(g + 1) * GH], prod[:, g, t * P:(t + 1) * P],
                                                head_ones[:, :], start=True, stop=True)
                last.then_inc(s_done, 1)

            over_batches(pe, batch)


def attend(nc, qs, ks, vs, att):
    ctx = ExitStack()
    with ctx:
        def sb(name, shape, dt=F32):
            return ctx.enter_context(nc.sbuf_tensor(name, shape, dt))

        def pb(name, shape, dt=F32):
            return ctx.enter_context(nc.psum_tensor(name, shape, dt))

        def sem(name):
            return ctx.enter_context(nc.semaphore(name))

        def two(make, name, *a):
            return [make(f"{name}{i}", *a) for i in range(2)]

        ROWS = 2 * HD
        qa = two(sb, "qa", [P, N], BF16)
        qb = two(sb, "qb", [P, N], BF16)
        ka = two(sb, "ka", [P, N], BF16)
        kb = two(sb, "kb", [P, N], BF16)
        shift_in = two(sb, "shift_in", [P, T])
        qa2 = two(sb, "qa2_", [P, N], BF16)
        qb2 = two(sb, "qb2_", [P, N], BF16)
        ka2 = two(sb, "ka2_", [P, N], BF16)
        kb2 = two(sb, "kb2_", [P, N], BF16)
        zrow = two(sb, "zrow", [P, N], BF16)
        ones3 = sb("ones3", [P, P], BF16)
        v_in = two(sb, "v_in", [P, T * VW])
        Z = two(sb, "Z", [P, T, N])
        top = sb("top", [P, T])
        shift = two(sb, "shift", [P, T])
        peak = two(sb, "peak", [P, T])
        sign_out = two(sb, "sign_out", [P, N], BF16)
        acc = sb("acc", [P, T])
        tneg = two(sb, "tneg", [P, T])
        step = sb("step", [P, T])
        e_old, e_new, e_sq = sb("e_old", [P, T]), sb("e_new", [P, T]), sb("e_sq", [P, T])
        move, opposite, same = sb("move", [P, T]), sb("opposite", [P, T]), sb("same", [P, T])
        num, den = sb("num", [P, T]), sb("den", [P, T])
        above_keep, side, side_t = sb("above_keep", [P, T]), sb("side", [P, T]), sb("side_t", [P, T])
        t_side, minus_one = sb("t_side", [P, T]), sb("minus_one", [P, T])
        half_c = sb("half_c", [P, T])
        ge_out = two(sb, "ge_out", [P, N], BF16)
        cnt = sb("cnt", [P, T])
        tC = sb("tC", [P, T])
        lo, hi = sb("lo", [P, T]), sb("hi", [P, T])
        err, miss, wide, tol = sb("err", [P, T]), sb("miss", [P, T]), sb("wide", [P, T]), sb("tol", [P, T])
        tnew, edge = sb("tnew", [P, T]), sb("edge", [P, T])
        pick = sb("pick", [P, T], I32)
        bad_col = sb("bad_col", [P, HD])
        bad_row = sb("bad_row", [P, HD])
        bad_max = sb("bad_max", [P, 1])
        bad_int = sb("bad_int", [P, 1], I32)
        YRING = 4
        Y = [sb(f"Y{i}", [P, N]) for i in range(YRING)]
        cand = sb("cand", [P, T, 9])
        iota9 = sb("iota9", [P, T, 9])
        rank, sel = sb("rank", [P, T]), sb("sel", [P, T, 9])
        sel2 = sb("sel2", [P, T, 9])
        near = sb("near", [P, T])
        aug = sb("aug", [P, 2, T])
        aug_rest = sb("aug_rest", [P, 2, T])
        aug_parts = sb("aug_parts", [P, 2, PARTS, T], BF16)
        AUGW = 2 * PARTS * T
        identb = sb("identb", [P, P], BF16)
        augT = sb("augT", [AUGW, P], BF16)
        E = [sb(f"E{j}", [P, HALF]) for j in range(BY_MASK)]
        R = two(sb, "R", [P, HALF], BF16)
        minus_identb = sb("minus_identb", [P, P], BF16)
        minus_ones3 = sb("minus_ones3", [P, P], BF16)
        PR = two(sb, "PR", [P, HALF])
        oT = sb("oT", [VW, N])
        ident = sb("ident", [P, P])
        rden = sb("rden", [P, T])
        at = two(sb, "at", [P, T, HD])

        ps_s = two(pb, "ps_s", [P, N])
        DB = 3
        ps_d = [pb(f"ps_d{i}", [P, HALF]) for i in range(DB)]
        ps_m = pb("ps_m", [P, HALF])
        ps_v = ps_m[0:VW, :]
        ps_o = ps_m[:, 0:T * VW].rearrange("p (t w) -> p t w", w=VW)
        ps_t = ps_m[0:AUGW, T * VW:T * VW + P // 2].bitcast(BF16)

        made = sem("made")
        a_loaded = two(lambda n: sem(n), "a_loaded")
        d_loaded = two(lambda n: sem(n), "d_loaded")
        rows_loaded = two(lambda n: sem(n), "rows_loaded")
        s_done = sem("s_done")
        evac_done = sem("evac_done")
        counted = sem("counted")
        t_ready = sem("t_ready")
        passed_dve = sem("passed_dve")
        passed_pool = sem("passed_pool")
        passed_pe = sem("passed_pe")
        exact = sem("exact")
        sided = sem("sided")
        y_ready = sem("y_ready")
        sel_ready = sem("sel_ready")
        near_ready = sem("near_ready")
        flag_ready = sem("flag_ready")
        picked = sem("picked")
        ranked = sem("ranked")
        aug_ready = sem("aug_ready")
        augT_done = sem("augT_done")
        augT_copied = sem("augT_copied")
        d_done = sem("d_done")
        first_done = sem("first_done")
        second_done = sem("second_done")
        exp_done = sem("exp_done")
        mask_done = sem("mask_done")
        pv_done = sem("pv_done")
        half_copied = sem("half_copied")
        turned = sem("turned")
        at_ready = sem("at_ready")
        at_stored = two(lambda n: sem(n), "at_stored")

        LOADS = 8
        BLK = NB * T
        SCORES_AFTER = (6, 7, 9, 10, 12, 13)
        D_FROM = 7
        R1_FROM = 5
        FIRST = 4
        UPD = ROUNDS + 1

        block = ctx.enter_context(nc.Block())

        def run(engine, iteration):
            for k in range(-1, FIRST):
                iteration(k, k % 2)
            pairs = (GROUPS - 1 - FIRST) // 2
            with engine.Fori(0, pairs) as i:
                iteration(2 * i + FIRST, 0, True)
                iteration(2 * i + FIRST + 1, 1, True)
            for k in range(FIRST + 2 * pairs, GROUPS + 2):
                iteration(k, k % 2)

        def stages(k, steady):
            if steady:
                return True, True, True, True
            return tuple(0 <= g < GROUPS for g in (k + 1, k, k - 1, k - 2))

        def turn(k, par, off, n):
            if isinstance(k, int):
                return (k + off) // 2 * n
            return (k + off - (par + off) % 2) * (n // 2)

        SUMMED = tuple(j for j in range(BLK) if j not in MASKED)
        BY_SUM = len(SUMMED)

        def wait_product_operand(engine, g, j):
            if j in MASKED:
                engine.wait_ge(mask_done, BY_MASK * g + MASKED.index(j) + 1)
            else:
                engine.wait_ge(exp_done, BY_SUM * g + SUMMED.index(j) + 1)

        @block.sync
        def _(sp):
            def load(q_a, q_b, k_a, k_b, g, loaded):
                q, k = qs[g], ks[g]
                sp.dma_start(q_a[0:64, :], q[0:2]).then_inc(loaded, 16)
                sp.dma_start(q_a[64:128, :], q[0:2]).then_inc(loaded, 16)
                sp.dma_start(k_a[0:64, :], k[0:2]).then_inc(loaded, 16)
                sp.dma_start(k_a[64:96, :], k[1]).then_inc(loaded, 16)
                sp.dma_start(k_a[96:128, :], k[0]).then_inc(loaded, 16)
                sp.dma_start(q_b[0:64, :], q[0:3:2]).then_inc(loaded, 16)
                sp.dma_start(k_b[0:32, :], k[2]).then_inc(loaded, 16)
                sp.dma_start(k_b[32:64, :], k[0]).then_inc(loaded, 16)

            def load_a(g, par):
                load(qa[par], qb[par], ka[par], kb[par], g, a_loaded[par])
                sp.dma_start(shift_in[par][:, :], vs[g, :, T * VW:VROW]).then_inc(a_loaded[par], 16)

            def load_d(g, par):
                load(qa2[par], qb2[par], ka2[par], kb2[par], g, d_loaded[par])
                sp.dma_start(v_in[par][:, :], vs[g, :, 0:T * VW]).then_inc(d_loaded[par], 16)

            sp.wait_ge(made, 1)
            load_a(0, 0)

            def iteration(k, par, steady=False):
                do_a, do_b, do_c, do_d = stages(k, steady)
                if do_d:
                    sp.wait_ge(augT_copied, k - 1)
                    sp.dma_start(qb2[par][ROWS:ROWS + PARTS, :], augT[0:PARTS * T, :]).then_inc(rows_loaded[par], 16)
                    sp.dma_start(zrow[par][0:PARTS, :], augT[PARTS * T:AUGW, :]).then_inc(rows_loaded[par], 16)
                if steady or (0 <= k + 2 < GROUPS and k + 2 >= 1):
                    if steady or k >= 0:
                        sp.wait_ge(s_done, T * (k + 1))
                        sp.wait_ge(t_ready, UPD * k + 1)
                    load_a(k + 2, par)
                if do_c:
                    if steady or k - 3 >= 0:
                        sp.wait_ge(pv_done, BLK * (k - 2))
                    load_d(k - 1, 1 - par)
                if do_d:
                    sp.wait_ge(at_ready, k - 1)
                    sp.dma_start(att[k - 2].rearrange("(t p) d -> p t d", p=P), at[par][:, :, :]).then_inc(at_stored[par], 16)

            run(sp, iteration)
            for q in range(2):
                sp.wait_ge(at_stored[q], 16 * (GROUPS // 2))

        @block.gpsimd
        def _(pool):
            nc.gpsimd.memset(ident[:, :], 1.0)
            nc.gpsimd.memset(identb[:, :], 1.0)
            pool.drain()
            nc.gpsimd.affine_select(out=ident[:, :], in_=ident[:, :], compare_op=ALU.is_equal, fill=0.0, base=0,
                                    pattern=[[-1, P]], channel_multiplier=1)
            nc.gpsimd.affine_select(out=identb[:, :], in_=identb[:, :], compare_op=ALU.is_equal, fill=0.0, base=0,
                                    pattern=[[-1, P]], channel_multiplier=1)
            nc.gpsimd.memset(ones3[:, :], 1.0)
            nc.gpsimd.memset(minus_ones3[:, :], -1.0)
            pool.drain()
            nc.gpsimd.tensor_scalar(minus_identb[:, :], identb[:, :], -1.0, None, ALU.mult)
            nc.gpsimd.memset(half_c[:, :], float(KEEP))
            nc.gpsimd.memset(minus_one[:, :], -1.0)
            nc.gpsimd.memset(cand[:, :, 0:1], 0.0)
            for q in range(2):
                for x in (qb[q], kb[q], qb2[q], kb2[q]):
                    pool.drain()
                    nc.gpsimd.memset(x[ROWS:P, :], 0.0)
                pool.drain()
                nc.gpsimd.memset(zrow[q][:, :], 0.0)
                pool.drain()
                nc.gpsimd.memset(kb2[q][ROWS:ROWS + PARTS, :], 1.0)
            pool.drain()
            for i in range(9):
                nc.gpsimd.memset(iota9[:, :, i:i + 1], float(i))
            nc.gpsimd.memset(bad_col[:, :], 0.0)
            pool.drain().then_inc(made, 1)

            def ts(out, in0, s1, s2=None, op0=ALU.mult, op1=ALU.bypass):
                nc.gpsimd.tensor_scalar(out[:, :], in0[:, :], s1, s2, op0, op1)
                pool.drain()

            def tt(out, in0, in1, op):
                nc.gpsimd.tensor_tensor(out[:, :], in0[:, :], in1[:, :], op)
                pool.drain()

            def iteration(k, par, steady=False):
                do_a, do_b, do_c, do_d = stages(k, steady)
                old = 1 - par

                def read_count(r, e):
                    pool.wait_ge(counted, T * (ROUNDS * k + r + 1))
                    pool.sem_inc(passed_pool, 1)
                    ts(e, acc, 0.5, N / 2 - KEEP, ALU.mult, ALU.add)
                    tt(move, e, step, ALU.mult)

                def move_t(e):
                    tt(e_sq, e, e, ALU.mult)
                    ts(e_sq, e_sq, WINDOW, None, ALU.is_gt)
                    tt(move, move, e_sq, ALU.mult)
                    nc.gpsimd.tensor_tensor(tneg[par][:, :], tneg[par][:, :], move[:, :], ALU.subtract)
                    pool.drain().then_inc(t_ready, 1)

                def distances(t):
                    n = T * (k - 1) + t
                    if steady or n >= YRING:
                        pool.wait_ge(ranked, n - YRING + 1)
                    pool.sem_inc(passed_pool, 1)
                    nc.gpsimd.tensor_scalar(Y[t % YRING][:, :], Z[old][:, t, :], side[:, t:t + 1], side_t[:, t:t + 1],
                                            ALU.mult, ALU.add).then_inc(y_ready, 1)

                def begin(q):
                    pool.wait_ge(evac_done, T * (k + 2))
                    pool.sem_inc(passed_pool, 1)
                    nc.gpsimd.tensor_scalar(shift[q][:, :], shift_in[q][:, :], 1.0, None, ALU.mult)
                    nc.gpsimd.tensor_scalar(peak[q][:, :], top[:, :], 1.0, None, ALU.mult)
                    nc.gpsimd.tensor_scalar(step[:, :], shift_in[q][:, :], SPACING, None, ALU.mult)
                    nc.gpsimd.tensor_scalar(tneg[q][:, :], shift_in[q][:, :], -1.0, None, ALU.mult)
                    pool.drain().then_inc(t_ready, 1)

                if do_b:
                    read_count(0, e_old)
                    move_t(e_old)
                if do_c:
                    pool.wait_ge(flag_ready, k)
                    pool.sem_inc(passed_pool, 1)
                    ts(above_keep, cnt, float(KEEP), None, ALU.is_gt)
                    ts(side, above_keep, -2.0, 1.0, ALU.mult, ALU.add)
                    ts(t_side, tC, BELOW)
                    tt(side_t, tC, t_side, ALU.subtract)
                    tt(side_t, side_t, above_keep, ALU.mult)
                    tt(t_side, t_side, side_t, ALU.add)
                    tt(side_t, t_side, side, ALU.mult)
                    ts(side_t, side_t, -1.0)
                    for t in range(T):
                        if t == YRING:
                            pool.wait_ge(exact, k)
                        distances(t)
                    ts(rank, cnt, -1.0, float(KEEP), ALU.mult, ALU.add)
                    tt(rank, rank, side, ALU.mult)
                    if steady or k >= 2:
                        pool.wait_ge(near_ready, k - 1)
                    nc.gpsimd.tensor_tensor(sel[:, :, :], iota9[:, :, :], rank[:, :].unsqueeze(2).broadcast_to([P, T, 9]),
                                            ALU.subtract)
                    pool.drain()
                    nc.gpsimd.tensor_scalar(sel2[:, :, :], sel[:, :, :], -0.5, None, ALU.add)
                    pool.drain()
                    nc.gpsimd.tensor_tensor(sel[:, :, :], sel2[:, :, :], sel2[:, :, :], ALU.mult)
                    pool.drain()
                    nc.gpsimd.tensor_scalar(sel2[:, :, :], sel[:, :, :], 0.25, 0.5, ALU.is_equal, ALU.mult)
                    pool.drain().then_inc(sel_ready, 1)
                    nc.gpsimd.tensor_tensor(aug[:, 0, :], shift[old][:, :], peak[old][:, :], ALU.subtract)
                    nc.gpsimd.tensor_scalar(aug[:, 1, :], peak[old][:, :], 1.0 + TINY, None, ALU.mult)
                    pool.drain()
                if do_b:
                    read_count(1, e_new)
                    tt(opposite, e_old, e_new, ALU.mult)
                    ts(opposite, opposite, 0.0, None, ALU.is_lt)
                    ts(same, opposite, -1.0, 1.0, ALU.mult, ALU.add)
                    tt(num, e_old, opposite, ALU.mult)
                    tt(den, e_new, opposite, ALU.mult)
                    tt(num, num, same, ALU.add)
                    tt(den, num, den, ALU.subtract)
                    tt(num, num, den, ALU.mult)
                    tt(den, den, den, ALU.mult)
                    tt(den, den, minus_one, ALU.pow)
                    tt(num, num, den, ALU.mult)
                    tt(move, move, num, ALU.mult)
                    move_t(e_new)
                if do_a:
                    begin(old)
                if do_c:
                    pool.wait_ge(near_ready, k)
                    pool.sem_inc(passed_pool, 1)
                    tt(near, near, side, ALU.mult)
                    tt(near, near, t_side, ALU.add)
                    nc.gpsimd.tensor_tensor(aug[:, 1, :], aug[:, 1, :], near[:, :], ALU.subtract)
                    pool.drain()
                    if steady or k >= 2:
                        pool.wait_ge(augT_done, k - 1)
                    pool.sem_inc(passed_pool, 1)
                    nc.gpsimd.tensor_copy(aug_parts[:, :, 0, :], aug[:, :, :])
                    pool.drain()
                    nc.gpsimd.tensor_tensor(aug_rest[:, :, :], aug[:, :, :], aug_parts[:, :, 0, :], ALU.subtract)
                    pool.drain()
                    nc.gpsimd.tensor_copy(aug_parts[:, :, 1, :], aug_rest[:, :, :])
                    pool.drain()
                    nc.gpsimd.tensor_tensor(aug_parts[:, :, 2, :], aug_rest[:, :, :], aug_parts[:, :, 1, :], ALU.subtract)
                    pool.drain().then_inc(aug_ready, 1)

            run(pool, iteration)

        @block.scalar
        def _(act):
            def iteration(k, par, steady=False):
                do_a, do_b, do_c, do_d = stages(k, steady)
                g = k - 2

                def count(r, t):
                    if t == 0:
                        act.wait_ge(t_ready, UPD * k + r + 1)
                    n = T * r + t
                    if steady or k > 0 or n >= 2:
                        act.wait_ge(counted, ROUNDS * T * k + n - 1)
                    nc.scalar.activation(sign_out[n % 2][:, :], Z[par][:, t, :], ACT.Sign, bias=tneg[par][:, t:t + 1],
                                         accum_out=acc[:, t:t + 1]).then_inc(counted, 1)

                def first(j):
                    act.wait_ge(d_done, BLK * g + j + 1)
                    if j in MASKED:
                        m = MASKED.index(j)
                        if steady or k > 2:
                            act.wait_ge(mask_done, BY_MASK * (g - 1) + m + 1)
                        nc.scalar.activation(E[m][:, :], ps_d[j % DB][:, :], ACT.Exp,
                                             scale=SCALE).then_inc(first_done, 1)
                    else:
                        if steady or k > 2 or j >= 2:
                            act.wait_ge(second_done, BLK * g + j - 1)
                        nc.scalar.activation(R[j % 2][:, :], ps_d[j % DB][:, :], ACT.Relu,
                                             scale=-FAR).then_inc(first_done, 1)

                def exponent(j):
                    act.wait_ge(second_done, BLK * g + j + 1)
                    if steady or k > 2 or j >= 2:
                        act.wait_ge(pv_done, BLK * g + j - 1)
                    nc.scalar.activation(PR[j % 2][:, :], ps_d[j % DB][:, :], ACT.Exp, scale=SCALE).then_inc(exp_done, 1)

                def copy_half(nh):
                    act.wait_ge(pv_done, BLK * g + T * (nh + 1))
                    if nh == 0 and (steady or k > 2):
                        act.wait_ge(turned, k - 2)
                    nc.scalar.copy(oT[:, nh * HALF:(nh + 1) * HALF], ps_v).then_inc(half_copied, 1)

                def block_of_d(j):
                    if j + 1 < BLK:
                        first(j + 1)
                    if j in SUMMED:
                        exponent(j)
                    if j == T:
                        copy_half(0)

                for t in range(T):
                    if do_b:
                        count(0, t)
                    if do_d and t == 1:
                        act.wait_ge(augT_done, k - 1)
                        if steady or k >= 3:
                            act.wait_ge(rows_loaded[1 - par], turn(k, par, -3, 32) + 32)
                        nc.scalar.copy(augT[:, :], ps_t).then_inc(augT_copied, 1)
                    if do_d and t == D_FROM - 1:
                        first(0)
                    if do_d and t >= D_FROM:
                        block_of_d(t - D_FROM)
                for j in range(T - D_FROM, BLK):
                    if do_d:
                        block_of_d(j)
                    if do_b and 0 <= j - R1_FROM < T:
                        count(1, j - R1_FROM)
                if do_d:
                    copy_half(1)

            run(act, iteration)

        @block.vector
        def _(dve):
            dve.wait_ge(made, 1)
            regs = [dve.alloc_register(f"bad_q{q}") for q in range(4)]
            bad = dve.alloc_register("bad")

            def iteration(k, par, steady=False):
                do_a, do_b, do_c, do_d = stages(k, steady)
                old = 1 - par

                def load_flag():
                    for q in range(4):
                        dve.load(regs[q], bad_int[HD * q:HD * q + 1, 0:1])
                    dve.reg_mov(bad, dve.snap(regs[0]) + dve.snap(regs[1]) + dve.snap(regs[2]) + dve.snap(regs[3]))

                def reduce_flag():
                    nc.vector.reduce_max(bad_col[:, 0:1], miss[:, :], AX_X)
                    dve.drain()
                    nc.vector.transpose(bad_row[:, :], bad_col[:, :])
                    dve.drain()
                    return nc.vector.reduce_max(bad_int[:, :], bad_row[:, :], AX_X)

                def exact_count(t):
                    if t >= 2 and t % 2 == 0:
                        dve.drain()
                    nc.vector.tensor_scalar(ge_out[t % 2][:, :], Z[old][:, t, :], tC[:, t:t + 1], None, ALU.is_ge, ALU.add,
                                            accum_out=cnt[:, t:t + 1])

                def judge():
                    nc.vector.tensor_scalar(err[:, :], cnt[:, :], -float(KEEP), None, ALU.add)
                    dve.drain()
                    nc.vector.tensor_tensor(miss[:, :], err[:, :], err[:, :], ALU.mult)
                    dve.drain()
                    nc.vector.tensor_scalar(miss[:, :], miss[:, :], WINDOW, None, ALU.is_gt)
                    dve.drain()

                def narrow():
                    nc.vector.tensor_scalar(pick[:, :], cnt[:, :], float(KEEP + REACH), None, ALU.is_gt)
                    dve.drain()
                    nc.vector.copy_predicated(lo[:, :], pick[:, :], tC[:, :])
                    dve.drain()
                    nc.vector.tensor_scalar(pick[:, :], cnt[:, :], float(KEEP - REACH), None, ALU.is_lt)
                    dve.drain()
                    nc.vector.copy_predicated(hi[:, :], pick[:, :], tC[:, :])
                    dve.drain()
                    nc.vector.tensor_tensor(wide[:, :], hi[:, :], lo[:, :], ALU.subtract)
                    dve.drain()

                def settle():
                    nc.vector.tensor_tensor(tnew[:, :], wide[:, :], tol[:, :], ALU.is_le)
                    dve.drain()
                    nc.vector.tensor_tensor(pick[:, :], tnew[:, :], miss[:, :], ALU.mult)
                    dve.drain()
                    nc.vector.copy_predicated(tC[:, :], pick[:, :], lo[:, :])
                    nc.vector.copy_predicated(cnt[:, :], pick[:, :], half_c[:, :])
                    dve.drain()
                    nc.vector.tensor_tensor(tnew[:, :], wide[:, :], tol[:, :], ALU.is_gt)
                    dve.drain()
                    nc.vector.tensor_tensor(miss[:, :], miss[:, :], tnew[:, :], ALU.mult)
                    dve.drain()

                def mend():
                    nc.vector.tensor_scalar(above_keep[:, :], cnt[:, :], float(KEEP), None, ALU.is_gt)
                    nc.vector.tensor_scalar(t_side[:, :], tC[:, :], BELOW, None, ALU.mult)
                    dve.drain()
                    nc.vector.tensor_scalar(side[:, :], above_keep[:, :], -2.0, 1.0, ALU.mult, ALU.add)
                    nc.vector.tensor_tensor(side_t[:, :], tC[:, :], t_side[:, :], ALU.subtract)
                    dve.drain()
                    nc.vector.tensor_tensor(side_t[:, :], side_t[:, :], above_keep[:, :], ALU.mult)
                    dve.drain()
                    nc.vector.tensor_tensor(t_side[:, :], t_side[:, :], side_t[:, :], ALU.add)
                    dve.drain()
                    nc.vector.tensor_tensor(side_t[:, :], t_side[:, :], side[:, :], ALU.mult)
                    dve.drain()
                    nc.vector.tensor_scalar(side_t[:, :], side_t[:, :], -1.0, None, ALU.mult)
                    dve.drain()
                    for t in range(YRING):
                        nc.vector.tensor_scalar(Y[t][:, :], Z[old][:, t, :], side[:, t:t + 1], side_t[:, t:t + 1],
                                                ALU.mult, ALU.add)
                    dve.drain()

                def search(newton):
                    if newton:
                        nc.vector.tensor_tensor(tnew[:, :], err[:, :], shift[old][:, :], ALU.mult)
                        dve.drain()
                        nc.vector.scalar_tensor_tensor(tnew[:, :], tnew[:, :], SPACING, tC[:, :], ALU.mult, ALU.add)
                        nc.vector.scalar_tensor_tensor(edge[:, :], wide[:, :], MARGIN, lo[:, :], ALU.mult, ALU.add)
                        dve.drain()
                        nc.vector.tensor_tensor(tnew[:, :], tnew[:, :], edge[:, :], ALU.max)
                        dve.drain()
                        nc.vector.scalar_tensor_tensor(edge[:, :], wide[:, :], 1.0 - MARGIN, lo[:, :], ALU.mult, ALU.add)
                        dve.drain()
                        nc.vector.tensor_tensor(tnew[:, :], tnew[:, :], edge[:, :], ALU.min)
                    else:
                        nc.vector.scalar_tensor_tensor(tnew[:, :], wide[:, :], 0.5, lo[:, :], ALU.mult, ALU.add)
                    nc.vector.tensor_copy(pick[:, :], miss[:, :])
                    dve.drain()
                    nc.vector.copy_predicated(tC[:, :], pick[:, :], tnew[:, :])
                    dve.drain()
                    for t in range(T):
                        exact_count(t)
                    dve.drain()
                    judge()
                    narrow()
                    settle()
                    reduce_flag()
                    dve.drain()
                    load_flag()

                def mask(j):
                    dve.wait_ge(second_done, BLK * (k - 2) + j + 1)
                    if steady or k > 2 or j >= 2:
                        dve.wait_ge(pv_done, BLK * (k - 2) + j - 1)
                    nc.vector.scalar_tensor_tensor(PR[j % 2][:, :], ps_d[j % DB][:, :], 0.0, E[MASKED.index(j)][:, :],
                                                   ALU.is_ge, ALU.mult).then_inc(mask_done, 1)

                if do_c:
                    dve.wait_ge(t_ready, UPD * k)
                    nc.vector.tensor_scalar(tC[:, :], tneg[old][:, :], -1.0, None, ALU.mult)
                    dve.drain()
                    for t in range(T):
                        exact_count(t)
                    dve.drain()
                    judge()
                    reduce_flag().then_inc(flag_ready, 1)
                if do_d:
                    for j in MASKED[:2]:
                        mask(j)
                if do_c:
                    dve.wait_ge(flag_ready, k)
                    dve.sem_inc(passed_dve, 1)
                    load_flag()
                    with dve.If(dve.snap(bad) > 0):
                        dve.drain()
                        dve.wait_ge(y_ready, T * (k - 1) + YRING)
                        dve.sem_inc(passed_dve, 1)
                        nc.vector.tensor_scalar(lo[:, :], shift[old][:, :], 0.25, None, ALU.mult)
                        nc.vector.tensor_scalar(hi[:, :], shift[old][:, :], 1.75, None, ALU.mult)
                        nc.vector.tensor_scalar(tol[:, :], shift[old][:, :], TINY, None, ALU.mult)
                        dve.drain()
                        narrow()
                        with dve.While(lambda: dve.snap(bad) > 0):
                            search(True)
                            with dve.If(dve.snap(bad) > 0):
                                search(True)
                                with dve.If(dve.snap(bad) > 0):
                                    search(False)
                        mend()
                    dve.sem_inc(exact, 1)
                if do_d:
                    mask(MASKED[2])
                for t in range(T):
                    if do_c:
                        dve.wait_ge(y_ready, T * (k - 1) + t + 1)
                        y = Y[t % YRING]
                        nc.vector.scalar_tensor_tensor(y[:, :], y[:, :], -FAR, y[:, :], ALU.mult, ALU.min).then_inc(picked, 1)
                    if do_a:
                        dve.wait_ge(s_done, T * (k + 1) + t + 1)
                        if t == 0:
                            dve.wait_ge(a_loaded[old], turn(k, par, 1, 16 * (LOADS + 1)) + 16 * (LOADS + 1))
                            if steady or k >= 0:
                                dve.wait_ge(t_ready, UPD * k + 1)
                        nc.vector.tensor_scalar(Z[old][:, t, :], ps_s[t % 2][:, :], shift_in[old][:, t:t + 1], None,
                                                ALU.add, ALU.max, accum_out=top[:, t:t + 1]).then_inc(evac_done, 1)
                    if do_c:
                        dve.wait_ge(picked, T * (k - 1) + t + 1)
                        dve.sem_inc(passed_dve, 1)
                        nc.vector.max(cand[:, t, 1:9], Y[t % YRING][:, :]).then_inc(ranked, 1)
                    if do_d and t < BY_MASK - 3:
                        mask(MASKED[3 + t])
                if do_c:
                    dve.wait_ge(sel_ready, k)
                    dve.wait_ge(ranked, T * k)
                    nc.vector.tensor_tensor(sel[:, :, :], sel2[:, :, :], cand[:, :, :], ALU.mult)
                    dve.drain()
                    nc.vector.reduce_sum(near[:, :], sel[:, :, :], AX_X).then_inc(near_ready, 1)
                if do_d:
                    dve.wait_ge(turned, k - 1)
                    if steady or k - 4 >= 0:
                        dve.wait_ge(at_stored[par], turn(k, par, -2, 16))
                    nc.vector.reciprocal(rden[:, :], ps_o[:, :, HD])
                    dve.drain()
                    nc.vector.tensor_tensor(at[par][:, :, :], ps_o[:, :, 0:HD],
                                            rden[:, :].unsqueeze(2).broadcast_to([P, T, HD]), ALU.mult).then_inc(at_ready, 1)

            run(dve, iteration)

        @block.tensor
        def _(pe):
            pe.wait_ge(made, 1)

            def iteration(k, par, steady=False):
                do_a, do_b, do_c, do_d = stages(k, steady)
                new = 1 - par
                g = k - 2

                def scores(t):
                    if t == 0:
                        pe.wait_ge(a_loaded[new], turn(k, par, 1, 16 * (LOADS + 1)) + 16 * (LOADS + 1))
                    if steady or k >= 0 or t >= 2:
                        pe.wait_ge(evac_done, T * (k + 1) + t - 1)
                    for h in range(NB):
                        s = slice(h * HALF, (h + 1) * HALF)
                        nc.tensor.matmul(ps_s[t % 2][:, s], qa[new][:, t * P:(t + 1) * P], ka[new][:, s],
                                         start=True, stop=False)
                        last = nc.tensor.matmul(ps_s[t % 2][:, s], qb[new][:, t * P:(t + 1) * P], kb[new][:, s],
                                                start=False, stop=True)
                    last.then_inc(s_done, 1)

                def distance(j):
                    nh, t = j // T, j % T
                    s = slice(nh * HALF, (nh + 1) * HALF)
                    if j == 0:
                        pe.wait_ge(d_loaded[par], turn(k, par, -2, 16 * (LOADS + 1)) + 16 * (LOADS + 1))
                        pe.wait_ge(rows_loaded[par], turn(k, par, -2, 32) + 32)
                    if j >= DB:
                        wait_product_operand(pe, g, j - DB)
                    elif j == 0 and (steady or k > 2):
                        wait_product_operand(pe, g - 1, BLK - 1)
                    nc.tensor.matmul(ps_d[j % DB][:, :], ka2[par][:, t * P:(t + 1) * P], qa2[par][:, s],
                                     start=True, stop=False)
                    last = nc.tensor.matmul(ps_d[j % DB][:, :], kb2[par][:, t * P:(t + 1) * P], qb2[par][:, s],
                                            start=False, stop=(j in MASKED))
                    if j in SUMMED:
                        last = nc.tensor.matmul(ps_d[j % DB][:, :], ones3[:, :], zrow[par][:, s],
                                                start=False, stop=True)
                    last.then_inc(d_done, 1)

                def second(j):
                    s = slice(j // T * HALF, (j // T + 1) * HALF)
                    pe.wait_ge(first_done, BLK * g + j + 1)
                    if j in MASKED:
                        last = nc.tensor.matmul(ps_d[j % DB][:, :], ones3[:, :], zrow[par][:, s],
                                                start=False, stop=True, skip_group_check=True)
                    else:
                        nc.tensor.matmul(ps_d[j % DB][:, :], minus_ones3[:, :], zrow[par][:, s],
                                         start=False, stop=False, skip_group_check=True)
                        last = nc.tensor.matmul(ps_d[j % DB][:, :], minus_identb[:, :], R[j % 2][:, :],
                                                start=False, stop=True, skip_group_check=True)
                    last.then_inc(second_done, 1)

                def product(j):
                    nh, t = j // T, j % T
                    wait_product_operand(pe, g, j)
                    if j == T:
                        pe.wait_ge(half_copied, NB * g + 1)
                    nc.tensor.matmul(ps_v, v_in[par][:, t * VW:(t + 1) * VW], PR[j % 2][:, :],
                                     start=(t == 0), stop=(t == T - 1)).then_inc(pv_done, 1)

                if do_a:
                    scores(0)
                    scores(1)
                if do_d:
                    pe.wait_ge(aug_ready, k - 1)
                    if steady or k >= 3:
                        pe.wait_ge(at_ready, k - 2)
                        pe.wait_ge(augT_copied, k - 2)
                    pe.sem_inc(passed_pe, 1)
                    nc.tensor.transpose(ps_t, aug_parts[:, :, :, :].rearrange("p a i t -> p (a i t)"),
                                        identb[:, :]).then_inc(augT_done, 1)
                    for j in range(DB):
                        distance(j)
                for j in range(BLK):
                    if do_d:
                        second(j)
                        if j >= 1:
                            if j + 2 < BLK:
                                distance(j + 2)
                            product(j - 1)
                    if do_a and j in SCORES_AFTER:
                        scores(SCORES_AFTER.index(j) + 2)
                if do_d:
                    product(BLK - 1)
                    pe.wait_ge(half_copied, NB * g + NB)
                    pe.sem_inc(passed_pe, 1)
                    for t in range(T):
                        last = nc.tensor.transpose(ps_o[:, t, :], oT[:, t * P:(t + 1) * P], ident[0:VW, 0:VW])
                    last.then_inc(turned, 1)

            run(pe, iteration)


def finish(nc, x, att, Wo, bo, W_r, W_k, W_v, mu_r, mu_k, out):
    ctx = ExitStack()
    with ctx:
        def sb(name, shape, dt=F32):
            return ctx.enter_context(nc.sbuf_tensor(name, shape, dt))

        def sem(name):
            return ctx.enter_context(nc.semaphore(name))

        ident = sb("f_ident", [P, P])
        wo = sb("f_wo", [P, CH, D])
        w_in = [sb(f"f_w_in{i}", [P, CH, D]) for i in range(3)]
        wT = [sb(f"f_wT{i}", [P, CH, D]) for i in range(3)]
        bo_row = sb("f_bo", [P, D])
        mu = [sb(f"f_mu{i}", [P, CH]) for i in range(2)]
        omu = [sb(f"f_omu{i}", [P, CH]) for i in range(2)]
        exps = sb("f_exps", [P, T])
        x_in = sb("f_x", [P, T, D])
        a_in = sb("f_a", [P, T, D])
        aT = sb("f_aT", [P, CH, N])
        x2 = sb("f_x2", [P, T, D])
        bst = sb("f_bst", [P, T, 6])
        mv = sb("f_mv", [P, T, 2])
        var_eps = sb("f_var", [P, T])
        rstd = sb("f_rstd", [P, T])
        xn = sb("f_xn", [P, T, D])
        hT = sb("f_hT", [P, CH, N + 2])
        prev = [sb(f"f_prev{i}", [P, CH, N]) for i in range(2)]
        mix = [sb(f"f_mix{i}", [P, CH, N]) for i in range(2)]
        kact = sb("f_kact", [P, CH, N])
        gate = sb("f_gate", [P, T, D])
        res = sb("f_res", [P, T, D])

        tp = [ctx.enter_context(nc.psum_tensor(f"f_tp{i}", [P, HALF], F32)) for i in range(2)]
        pj = [ctx.enter_context(nc.psum_tensor(f"f_pj{i}", [P, HALF], F32)) for i in range(4)]

        weights = sem("f_weights")
        made = sem("f_made")
        wt_done = sem("f_wt_done")
        wt_taken = sem("f_wt_taken")
        omu_ready = sem("f_omu_ready")
        x_loaded = sem("f_x_loaded")
        a_loaded = sem("f_a_loaded")
        x_biased = sem("f_x_biased")
        tp_done = sem("f_tp_done")
        tp_taken = sem("f_tp_taken")
        pj_done = sem("f_pj_done")
        y_taken = sem("f_y_taken")
        stats = sem("f_stats")
        rstd_ready = sem("f_rstd_ready")
        xn_ready = sem("f_xn_ready")
        prev_ready = sem("f_prev_ready")
        mix_ready = sem("f_mix_ready")
        relu_done = sem("f_relu_done")
        k_taken = sem("f_k_taken")
        gate_exp = sem("f_gate_exp")
        v_taken = sem("f_v_taken")
        res_ready = sem("f_res_ready")
        stored = sem("f_stored")
        LOADS = 7
        block = ctx.enter_context(nc.Block())

        @block.sync
        def _(sp):
            sp.dma_start(wo[:, :, :], Wo.rearrange("(k p) d -> p k d", p=P)).then_inc(weights, 16)
            for w, src in zip(w_in, (W_r, W_k, W_v)):
                sp.dma_start(w[:, :, :], src.rearrange("(k p) d -> p k d", p=P)).then_inc(weights, 16)
            sp.dma_start(bo_row[:, :], bo.partition_broadcast(P)).then_inc(weights, 16)
            for m, src in zip(mu, (mu_r, mu_k)):
                sp.dma_start(m[:, :], src.rearrange("(k p) -> p k", p=P),
                             allow_slow_non_contiguous=True).then_inc(weights, 16)

            def load(b):
                sp.dma_start(a_in[:, :, :].rearrange("p t (h d) -> p t h d", h=H),
                             att[b].rearrange("h (t p) d -> p t h d", p=P)).then_inc(a_loaded, 16) if False else None
                for h in range(H):
                    sp.dma_start(a_in[:, :, h * HD:(h + 1) * HD],
                                 att[b, h].rearrange("(t p) d -> p t d", p=P)).then_inc(a_loaded, 16)
                sp.dma_start(x_in[:, :, :], x[b].rearrange("(t p) d -> p t d", p=P)).then_inc(x_loaded, 16)

            def store(b):
                sp.wait_ge(res_ready, b + 1)
                sp.dma_start(out[b].rearrange("(t p) d -> p t d", p=P), res[:, :, :]).then_inc(stored, 16)

            load(0)
            with sp.Fori(1, B) as b:
                wait(sp, y_taken, 4 * b)
                load(b)
                store(b - 1)
            store(B - 1)
            sp.wait_ge(stored, 16 * B)

        @block.gpsimd
        def _(pool):
            make_identity(pool, nc, ident, made)
            nc.gpsimd.memset(exps[:, :], -0.5)
            nc.gpsimd.memset(hT[:, :, 1:2], 0.0)
            pool.drain().then_inc(made, 1)
            pool.wait_ge(weights, 16 * LOADS)
            def batch(b):
                pool.wait_ge(x_loaded, 16 * b + 16)
                for t in range(T):
                    nc.gpsimd.tensor_tensor(x_in[:, t, :], x_in[:, t, :], bo_row[:, :], ALU.add)
                pool.drain().then_inc(x_biased, 1)
                pool.wait_ge(stats, b + 1)
                nc.gpsimd.tensor_tensor(rstd[:, :], var_eps[:, :], exps[:, :], ALU.pow).then_inc(rstd_ready, 1)

            over_batches(pool, batch)

        @block.vector
        def _(dve):
            dve.wait_ge(weights, 16 * LOADS)
            dve.wait_ge(made, 2)
            for i in range(2):
                nc.vector.tensor_scalar(omu[i][:, :], mu[i][:, :], -1.0, 1.0, ALU.mult, ALU.add)
            dve.drain().then_inc(omu_ready, 1)
            def batch(b):
                dve.wait_ge(x_biased, b + 1)
                wait(dve, res_ready, b)
                for u in range(4):
                    dve.wait_ge(pj_done, 16 * b + u + 1)
                    nc.vector.tensor_tensor(x2[:, 2 * u:2 * u + 2, :], x_in[:, 2 * u:2 * u + 2, :],
                                            pj[u % 4][:, :].rearrange("p (t d) -> p t d", t=2), ALU.add).then_inc(y_taken, 1)
                dve.drain()
                for t in range(T):
                    nc.vector.bn_stats(bst[:, t, :], x2[:, t, :])
                dve.drain()
                for t in range(T):
                    nc.vector.bn_aggr(mv[:, t, :], bst[:, t, :])
                dve.drain()
                nc.vector.tensor_scalar(var_eps[:, :], mv[:, :, 1], EPS, None, ALU.add).then_inc(stats, 1)
                dve.wait_ge(rstd_ready, b + 1)
                for t in range(T):
                    last = nc.vector.tensor_scalar(xn[:, t, :], x2[:, t, :], mv[:, t, 0:1], rstd[:, t:t + 1],
                                                   ALU.subtract, ALU.mult)
                last.then_inc(xn_ready, 1)
                for i in (1, 0):
                    dve.wait_ge(prev_ready, 2 * b + 2 - i)
                    for k in range(CH):
                        last = nc.vector.scalar_tensor_tensor(mix[i][:, k, :], hT[:, k, 2:N + 2], mu[i][:, k:k + 1],
                                                              prev[i][:, k, :], ALU.mult, ALU.add)
                    last.then_inc(mix_ready, 1)
                for g in range(CH):
                    for nh in range(NB):
                        u = 4 + g * NB + nh
                        s = slice(nh * HALF, (nh + 1) * HALF)
                        dve.wait_ge(relu_done, 4 * b + g * NB + nh + 1)
                        nc.vector.tensor_tensor(kact[:, g, s], kact[:, g, s], pj[u % 4][:, :], ALU.mult).then_inc(k_taken, 1)
                dve.wait_ge(gate_exp, 4 * b + 4)
                nc.vector.tensor_scalar(gate[:, :, :], gate[:, :, :], 1.0, None, ALU.add)
                dve.drain()
                nc.vector.reciprocal(gate[:, :, :], gate[:, :, :])
                dve.drain()
                wait(dve, stored, 16 * b)
                for i in range(4):
                    u = 12 + i
                    s = slice(2 * i, 2 * i + 2)
                    dve.wait_ge(pj_done, 16 * b + u + 1)
                    nc.vector.tensor_tensor(res[:, s, :], gate[:, s, :], pj[u % 4][:, :].rearrange("p (t d) -> p t d", t=2),
                                            ALU.mult).then_inc(v_taken, 1)
                dve.drain()
                nc.vector.tensor_tensor(res[:, :, :], res[:, :, :], x2[:, :, :], ALU.add).then_inc(res_ready, 1)

            over_batches(dve, batch)

        @block.scalar
        def _(act):
            act.wait_ge(omu_ready, 1)
            for i in range(3):
                act.wait_ge(wt_done, i + 1)
                nc.scalar.copy(wT[i][:, :, :], tp[i % 2][:, :].rearrange("p (k d) -> p k d", k=CH)).then_inc(wt_taken, 1)
            def batch(b):
                wait(act, pj_done, 16 * b)
                for k in range(CH):
                    for half in range(NB):
                        u = k * NB + half
                        act.wait_ge(tp_done, 8 * b + u + 1)
                        nc.scalar.copy(aT[:, k, half * HALF:(half + 1) * HALF], tp[u % 2][:, :]).then_inc(tp_taken, 1)
                wait(act, mix_ready, 2 * b)
                for k in range(CH):
                    for half in range(NB):
                        u = 4 + k * NB + half
                        act.wait_ge(tp_done, 8 * b + u + 1)
                        nc.scalar.copy(hT[:, k, 2 + half * HALF:2 + (half + 1) * HALF], tp[u % 2][:, :]).then_inc(tp_taken, 1)
                act.wait_ge(tp_taken, 8 * b + 8)
                for i in (1, 0):
                    for k in range(CH):
                        last = nc.scalar.activation(prev[i][:, k, :], hT[:, k, 1:N + 1], ACT.Identity,
                                                    scale=omu[i][:, k:k + 1])
                    last.then_inc(prev_ready, 1)
                for g in range(CH):
                    for nh in range(NB):
                        u = 4 + g * NB + nh
                        act.wait_ge(pj_done, 16 * b + u + 1)
                        nc.scalar.activation(kact[:, g, nh * HALF:(nh + 1) * HALF], pj[u % 4][:, :], ACT.Relu).then_inc(relu_done, 1)
                for i in range(4):
                    u = 8 + i
                    act.wait_ge(pj_done, 16 * b + u + 1)
                    nc.scalar.activation(gate[:, 2 * i:2 * i + 2, :], pj[u % 4][:, :].rearrange("p (t d) -> p t d", t=2),
                                         ACT.Exp, scale=-1.0).then_inc(gate_exp, 1)

            over_batches(act, batch)

        @block.tensor
        def _(pe):
            pe.wait_ge(weights, 16 * LOADS)
            pe.wait_ge(made, 2)
            for i in range(3):
                if i == 2:
                    pe.wait_ge(wt_taken, 1)
                for k in range(CH):
                    for dch in range(CH):
                        last = nc.tensor.transpose(tp[i % 2][:, k * D + dch * P:k * D + (dch + 1) * P],
                                                   w_in[i][:, dch, k * P:(k + 1) * P], ident[:, :])
                last.then_inc(wt_done, 1)
            pe.wait_ge(wt_taken, 3)
            def batch(b):
                def transposes(unit0, source):
                    for k in range(CH):
                        for half in range(NB):
                            u = unit0 + k * NB + half
                            if u >= 2:
                                pe.wait_ge(tp_taken, 8 * b + u - 1)
                            else:
                                wait(pe, tp_taken, 8 * b)
                            for i in range(4):
                                last = nc.tensor.transpose(tp[u % 2][:, i * P:(i + 1) * P], source(k, half * 4 + i),
                                                           ident[:, :])
                            last.then_inc(tp_done, 1)

                def natural(u0, lhs, w, free):
                    for i in range(4):
                        free(i)
                        for t2 in range(2):
                            t = 2 * i + t2
                            for k in range(CH):
                                last = nc.tensor.matmul(pj[i][:, t2 * D:(t2 + 1) * D], lhs[:, k, t * P:(t + 1) * P],
                                                        w[:, k, :], start=(k == 0), stop=(k == CH - 1))
                        last.then_inc(pj_done, 1)

                pe.wait_ge(a_loaded, 16 * H * b + 16 * H)
                transposes(0, lambda k, t: a_in[:, t, k * P:(k + 1) * P])
                pe.wait_ge(tp_taken, 8 * b + 4)
                natural(0, aT, wo, lambda i: wait(pe, v_taken, 4 * b))
                pe.wait_ge(xn_ready, b + 1)
                transposes(4, lambda k, t: xn[:, t, k * P:(k + 1) * P])
                pe.wait_ge(mix_ready, 2 * b + 1)
                for g in range(CH):
                    for nh in range(NB):
                        u = 4 + g * NB + nh
                        pe.wait_ge(y_taken, 4 * b + g * NB + nh + 1)
                        for k in range(CH):
                            last = nc.tensor.matmul(pj[u % 4][:, :], wT[1][:, k, g * P:(g + 1) * P],
                                                    mix[1][:, k, nh * HALF:(nh + 1) * HALF],
                                                    start=(k == 0), stop=(k == CH - 1))
                        last.then_inc(pj_done, 1)
                pe.wait_ge(mix_ready, 2 * b + 2)
                natural(8, mix[0], wT[0], lambda i: pe.wait_ge(k_taken, 4 * b + i + 1))
                natural(12, kact, wT[2], lambda i: pe.wait_ge(gate_exp, 4 * b + i + 1))

            over_batches(pe, batch)


def program(nc, x, Wq, bq, Wk, bk, Wv, bv, Wo, bo, W_r, W_k, W_v, mu_r, mu_k, out):
    qs = nc.dram_tensor("q_parts", [B, CH, GH, PARTS, HD, N], BF16, kind="Internal").ap()
    ks = nc.dram_tensor("k_parts", [B, CH, GH, PARTS, HD, N], BF16, kind="Internal").ap()
    vs = nc.dram_tensor("v_ones", [B, H, P, VROW], F32, kind="Internal").ap()
    att = nc.dram_tensor("att", [B, H, N, HD], F32, kind="Internal").ap()
    project(nc, x, Wq, bq, Wk, bk, Wv, bv, qs, ks, vs)
    attend(nc, qs.rearrange("b c h i d n -> (b c h) i d n"), ks.rearrange("b c h i d n -> (b c h) i d n"),
           vs.rearrange("b h p w -> (b h) p w"), att.rearrange("b h n d -> (b h) n d"))
    finish(nc, x, att, Wo, bo, W_r, W_k, W_v, mu_r, mu_k, out)


_INS = ['L0_attn_x', 'L0_attn_Wq', 'L0_attn_bq', 'L0_attn_Wk', 'L0_attn_bk', 'L0_attn_Wv', 'L0_attn_bv',
        'L0_attn_Wo', 'L0_attn_bo', 'L0_ffn_W_r', 'L0_ffn_W_k', 'L0_ffn_W_v', 'L0_ffn_mu_r', 'L0_ffn_mu_k']


def kernel(**inputs):
    import numpy as _np
    import concourse.bacc as _bacc
    from concourse import mybir as _mybir
    from concourse.bass_utils import run_bass_kernel_spmd as _run

    nc = _bacc.Bacc("TRN2", target_bir_lowering=False, num_devices=1)
    arrays, args = {}, []
    for name in _INS:
        a = _np.ascontiguousarray(inputs[name])
        arrays[f"in_{name}_dram"] = a
        args.append(nc.dram_tensor(f"in_{name}_dram", a.shape, _mybir.dt.from_np(a.dtype), kind="ExternalInput").ap())
    out = nc.dram_tensor("out_dram", (16, 1024, 256), _mybir.dt.float32, kind="ExternalOutput").ap()
    program(nc, *args, out)
    r = _run(nc, [arrays], core_ids=[0])
    return r.results[0]["out_dram"]
```

```python
import concourse.bass as bass
from concourse import mybir
from contextlib import ExitStack

F32 = mybir.dt.float32
BF16 = mybir.dt.bfloat16
I32 = mybir.dt.int32
ALU = mybir.AluOpType
ACT = mybir.ActivationFunctionType
AX_X = mybir.AxisListType.X

P = 128
B, N, D = 16, 1024, 256
H, HD = 8, 32
KEEP = N // 2
T = N // P
CH = D // P
GH = P // HD
GROUPS = B * H
HALF = N // 2
NB = N // HALF
PARTS = 3
VW = HD + 1
VROW = T * VW + T
EPS = 1e-5
SCALE = float(HD) ** -0.5
RIDGE = 4e-6
SPACING = 0.5 * (2.0 * 3.141592653589793) ** 0.5 / N
REACH = 7
WINDOW = REACH ** 2 + 0.5
TINY = 2.0 ** -21
BELOW = 1.0 - 2.0 ** -24
FAR = 1e20
CAUTION = 0.75
MARGIN = 2.0 ** -10
ROUNDS = 2
MASKED = (2, 3, 4)
BY_MASK = len(MASKED)


def wait(engine, semaphore, value):
    if not isinstance(value, int) or value > 0:
        engine.wait_ge(semaphore, value)


def over_batches(engine, batch, ahead=False):
    batch(0)
    if not ahead:
        with engine.Fori(1, B) as b:
            batch(b)
    else:
        if B > 2:
            with engine.Fori(1, B - 1) as b:
                batch(b)
        batch(B - 1, more=False)


def make_identity(pool, nc, ident, made):
    nc.gpsimd.memset(ident[:, :], 1.0)
    pool.drain()
    nc.gpsimd.affine_select(out=ident[:, :], in_=ident[:, :], compare_op=ALU.is_equal, fill=0.0, base=0,
                            pattern=[[-1, P]], channel_multiplier=1).then_inc(made, 1)


def project(nc, x, Wq, bq, Wk, bk, Wv, bv, qs, ks, vs):
    ctx = ExitStack()
    with ctx:
        def sb(name, shape, dt=F32):
            return ctx.enter_context(nc.sbuf_tensor(name, shape, dt))

        def sem(name):
            return ctx.enter_context(nc.semaphore(name))

        ident = sb("p_ident", [P, P])
        spread_mask = sb("p_spread_mask", [P, P])
        head_ones = sb("p_head_ones", [P, CH, H])
        sT = sb("p_sT", [H, N])
        wq = sb("p_wq", [P, CH, D])
        wk = sb("p_wk", [P, CH, D])
        wv = sb("p_wv", [P, CH, D])
        bq_col = sb("p_bq", [P, CH])
        bk_col = sb("p_bk", [P, CH])
        bv_row = sb("p_bv", [P, D])
        exps = sb("p_exps", [P, T])
        xt = sb("p_x", [P, T, D])
        bst = sb("p_bst", [P, T, 6])
        mv = sb("p_mv", [P, T, 2])
        var_eps = sb("p_var", [P, T])
        rstd = sb("p_rstd", [P, T])
        xn = sb("p_xn", [P, T, D])
        xT = sb("p_xT", [P, CH, N])
        qT = sb("p_qT", [P, CH, N])
        kT = sb("p_kT", [P, CH, N])
        ksum = sb("p_ksum", [P, CH, NB])
        kmean = sb("p_kmean", [P, CH])
        qrest = sb("p_qrest", [P, CH, N])
        krest = sb("p_krest", [P, CH, N])
        qp = sb("p_qp", [P, PARTS, CH, N], BF16)
        kp = sb("p_kp", [P, PARTS, CH, N], BF16)
        knat = sb("p_knat", [P, T, D])
        cm = sb("p_cm", [P, CH, P])
        prod = sb("p_prod", [P, CH, N])
        sq = sb("p_sq", [P, H, T])
        va = sb("p_va", [P, H, VROW])
        v_view = va[:, :, 0:T * VW].rearrange("p h (t w) -> p h t w", w=VW)
        shift_view = va[:, :, T * VW:VROW]

        tp = [ctx.enter_context(nc.psum_tensor(f"p_tp{i}", [P, HALF], F32)) for i in range(2)]
        pj = [ctx.enter_context(nc.psum_tensor(f"p_pj{i}", [P, HALF], F32)) for i in range(4)]
        ps_c = ctx.enter_context(nc.psum_tensor("p_ps_c", [P, CH, P], F32))
        ps_s = ctx.enter_context(nc.psum_tensor("p_ps_s", [P, T, H], F32))

        weights = sem("p_weights")
        made = sem("p_made")
        x_loaded = sem("p_x_loaded")
        stats = sem("p_stats")
        rstd_ready = sem("p_rstd_ready")
        xn_ready = sem("p_xn_ready")
        tp_done = sem("p_tp_done")
        tp_taken = sem("p_tp_taken")
        pj_done = sem("p_pj_done")
        q_taken = sem("p_q_taken")
        k_taken = sem("p_k_taken")
        v_taken = sem("p_v_taken")
        w_taken = sem("p_w_taken")
        k_centred = sem("p_k_centred")
        q_high = sem("p_q_high")
        q_rest = sem("p_q_rest")
        q_mid = sem("p_q_mid")
        q_low = sem("p_q_low")
        k_high = sem("p_k_high")
        k_rest = sem("p_k_rest")
        k_mid = sem("p_k_mid")
        k_low = sem("p_k_low")
        c_done = sem("p_c_done")
        c_taken = sem("p_c_taken")
        sums_done = sem("p_sums_done")
        sums_taken = sem("p_sums_taken")
        passed_pe = sem("p_passed_pe")
        s_done = sem("p_s_done")
        s_taken = sem("p_s_taken")
        shift_ready = sem("p_shift_ready")
        q_stored = sem("p_q_stored")
        k_stored = sem("p_k_stored")
        v_stored = sem("p_v_stored")

        LOADS = 6
        MADE = 3
        block = ctx.enter_context(nc.Block())

        @block.sync
        def _(sp):
            for w, src in ((wq, Wq), (wk, Wk), (wv, Wv)):
                sp.dma_start(w[:, :, :], src.rearrange("(k p) d -> p k d", p=P)).then_inc(weights, 16)
            sp.dma_start(bq_col[:, :], bq.rearrange("(k p) -> p k", p=P),
                             allow_slow_non_contiguous=True).then_inc(weights, 16)
            sp.dma_start(bk_col[:, :], bk.rearrange("(k p) -> p k", p=P),
                             allow_slow_non_contiguous=True).then_inc(weights, 16)
            sp.dma_start(bv_row[:, :], bv.partition_broadcast(P)).then_inc(weights, 16)
            sp.dma_start(xt[:, :, :], x[0].rearrange("(t p) d -> p t d", p=P)).then_inc(x_loaded, 16)

            def store(b):
                sp.wait_ge(q_low, b + 1)
                sp.wait_ge(q_mid, b + 1)
                for c in range(CH):
                    for i in range(PARTS):
                        sp.dma_start(qs[b, c, :, i, :, :], qp[:, i, c, :]).then_inc(q_stored, 16)
                sp.wait_ge(k_low, b + 1)
                sp.wait_ge(k_mid, b + 1)
                for c in range(CH):
                    for i in range(PARTS):
                        sp.dma_start(ks[b, c, :, i, :, :], kp[:, i, c, :]).then_inc(k_stored, 16)
                sp.wait_ge(shift_ready, b + 1)
                sp.wait_ge(v_taken, 4 * b + 4)
                sp.dma_start(vs[b].rearrange("h p w -> p h w"), va[:, :, :]).then_inc(v_stored, 16)


            def load(b):
                sp.wait_ge(xn_ready, b)
                sp.dma_start(xt[:, :, :], x[b].rearrange("(t p) d -> p t d", p=P)).then_inc(x_loaded, 16)

            load(1)
            with sp.Fori(2, B) as b:
                store(b - 2)
                load(b)
            store(B - 2)
            store(B - 1)
            sp.wait_ge(q_stored, 16 * CH * PARTS * B)
            sp.wait_ge(k_stored, 16 * CH * PARTS * B)
            sp.wait_ge(v_stored, 16 * B)

        @block.gpsimd
        def _(pool):
            make_identity(pool, nc, ident, made)
            nc.gpsimd.memset(exps[:, :], -0.5)
            nc.gpsimd.memset(v_view[:, :, :, HD:VW], 1.0)
            nc.gpsimd.memset(head_ones[:, :, :], 0.0)
            pool.wait_ge(made, 1)
            nc.gpsimd.tensor_scalar(spread_mask[:, :], ident[:, :], RIDGE / N, None, ALU.mult)
            pool.drain()
            for i in range(GH):
                s = slice(i * HD, (i + 1) * HD)
                for g in range(CH):
                    nc.gpsimd.memset(head_ones[s, g, g * GH + i:g * GH + i + 1], 1.0)
                nc.gpsimd.tensor_scalar(spread_mask[s, s], spread_mask[s, s], 1.0 / N, None, ALU.add)
            pool.drain().then_inc(made, 1)


            def inverse_root(b):
                pool.wait_ge(stats, b + 1)
                nc.gpsimd.tensor_tensor(rstd[:, :], var_eps[:, :], exps[:, :], ALU.pow).then_inc(rstd_ready, 1)

            def batch(b, more=True):
                pool.wait_ge(q_high, b + 1)
                nc.gpsimd.tensor_tensor(qrest[:, :, :], qT[:, :, :], qp[:, 0, :, :], ALU.subtract).then_inc(q_rest, 1)
                if more:
                    inverse_root(b + 1)
                pool.wait_ge(q_mid, b + 1)
                nc.gpsimd.tensor_tensor(qp[:, 2, :, :], qrest[:, :, :], qp[:, 1, :, :], ALU.subtract).then_inc(q_low, 1)

            inverse_root(0)
            over_batches(pool, batch, ahead=True)

        @block.vector
        def _(dve):
            dve.wait_ge(weights, 16 * LOADS)
            dve.wait_ge(made, 2)

            def row_statistics(b):
                dve.wait_ge(x_loaded, 16 * b + 16)
                for t in range(T):
                    nc.vector.bn_stats(bst[:, t, :], xt[:, t, :])
                dve.drain()
                for t in range(T):
                    nc.vector.bn_aggr(mv[:, t, :], bst[:, t, :])
                dve.drain()
                nc.vector.tensor_scalar(var_eps[:, :], mv[:, :, 1], EPS, None, ALU.add).then_inc(stats, 1)

            def normalise(b):
                dve.wait_ge(rstd_ready, b + 1)
                wait(dve, tp_done, 8 * b - 4)
                for t in range(T):
                    last = nc.vector.tensor_scalar(xn[:, t, :], xt[:, t, :], mv[:, t, 0:1], rstd[:, t:t + 1],
                                                   ALU.subtract, ALU.mult)
                last.then_inc(xn_ready, 1)

            def batch(b, more=True):
                for g in range(CH):
                    for nh in range(NB):
                        u = 4 + g * NB + nh
                        dve.wait_ge(pj_done, 16 * b + u + 1)
                        nc.vector.tensor_scalar(kT[:, g, nh * HALF:(nh + 1) * HALF], pj[u % 4][:, :],
                                                bk_col[:, g:g + 1], 0.0, ALU.add, ALU.add,
                                                accum_out=ksum[:, g, nh:nh + 1]).then_inc(k_taken, 1)
                dve.drain()
                nc.vector.tensor_tensor(kmean[:, :], ksum[:, :, 0], ksum[:, :, 1], ALU.add)
                dve.drain()
                nc.vector.tensor_scalar(kmean[:, :], kmean[:, :], 1.0 / N, None, ALU.mult)
                dve.drain()
                for g in range(CH):
                    last = nc.vector.tensor_scalar(kT[:, g, :], kT[:, g, :], kmean[:, g:g + 1], None, ALU.subtract)
                last.then_inc(k_centred, 1)
                wait(dve, v_stored, 16 * b)
                for i in range(4):
                    u = 8 + i
                    dve.wait_ge(pj_done, 16 * b + u + 1)
                    for t2 in range(2):
                        last = nc.vector.tensor_tensor(
                            v_view[:, :, 2 * i + t2, 0:HD],
                            pj[u % 4][:, t2 * D:(t2 + 1) * D].rearrange("p (h d) -> p h d", h=H),
                            bv_row[:, :].rearrange("p (h d) -> p h d", h=H), ALU.add)
                    last.then_inc(v_taken, 1)
                if more:
                    row_statistics(b + 1)
                dve.wait_ge(k_high, b + 1)
                nc.vector.tensor_tensor(krest[:, :, :], kT[:, :, :], kp[:, 0, :, :], ALU.subtract).then_inc(k_rest, 1)
                dve.wait_ge(c_done, b + 1)
                for g in range(CH):
                    last = nc.vector.tensor_tensor(cm[:, g, :], ps_c[:, g, :], spread_mask[:, :], ALU.mult)
                last.then_inc(c_taken, 1)
                dve.wait_ge(k_mid, b + 1)
                nc.vector.tensor_tensor(kp[:, 2, :, :], krest[:, :, :], kp[:, 1, :, :], ALU.subtract).then_inc(k_low, 1)
                for g in range(CH):
                    for nh in range(NB):
                        u = 12 + g * NB + nh
                        s = slice(nh * HALF, (nh + 1) * HALF)
                        dve.wait_ge(pj_done, 16 * b + u + 1)
                        nc.vector.tensor_tensor(prod[:, g, s], pj[u % 4][:, :], qT[:, g, s], ALU.mult).then_inc(w_taken, 1)
                if more:
                    normalise(b + 1)
                dve.wait_ge(s_done, b + 1)
                dve.wait_ge(s_done, b + 1)
                wait(dve, shift_ready, b)
                nc.vector.tensor_scalar(sq[:, :, :], ps_s[:, :, :].rearrange("p t h -> p h t"), 4.0, 0.0,
                                        ALU.mult, ALU.max).then_inc(s_taken, 1)

            row_statistics(0)
            normalise(0)
            over_batches(dve, batch, ahead=True)

        @block.scalar
        def _(act):
            act.wait_ge(weights, 16 * LOADS)

            def shifts(b):
                act.wait_ge(s_taken, b + 1)
                nc.scalar.activation(shift_view, sq[:, :, :], ACT.Sqrt).then_inc(shift_ready, 1)

            def batch(b):
                wait(act, pj_done, 16 * b)
                for k in range(CH):
                    for half in range(NB):
                        u = k * NB + half
                        act.wait_ge(tp_done, 8 * b + u + 1)
                        nc.scalar.copy(xT[:, k, half * HALF:(half + 1) * HALF], tp[u % 2][:, :]).then_inc(tp_taken, 1)
                if not isinstance(b, int):
                    shifts(b - 1)
                wait(act, q_stored, 16 * CH * PARTS * b)
                wait(act, w_taken, 4 * b)
                for g in range(CH):
                    for nh in range(NB):
                        u = g * NB + nh
                        act.wait_ge(pj_done, 16 * b + u + 1)
                        nc.scalar.activation(qT[:, g, nh * HALF:(nh + 1) * HALF], pj[u % 4][:, :], ACT.Identity,
                                             bias=bq_col[:, g:g + 1]).then_inc(q_taken, 1)
                act.wait_ge(q_taken, 4 * b + 4)
                nc.scalar.copy(qp[:, 0, :, :], qT[:, :, :]).then_inc(q_high, 1)
                act.wait_ge(k_centred, b + 1)
                wait(act, k_stored, 16 * CH * PARTS * b)
                nc.scalar.copy(kp[:, 0, :, :], kT[:, :, :]).then_inc(k_high, 1)
                for k in range(CH):
                    for half in range(NB):
                        u = 4 + k * NB + half
                        act.wait_ge(tp_done, 8 * b + u + 1)
                        nc.scalar.copy(knat[:, half * 4:half * 4 + 4, k * P:(k + 1) * P],
                                       tp[u % 2][:, :].rearrange("p (t d) -> p t d", t=4)).then_inc(tp_taken, 1)
                act.wait_ge(k_rest, b + 1)
                nc.scalar.copy(kp[:, 1, :, :], krest[:, :, :]).then_inc(k_mid, 1)
                act.wait_ge(q_rest, b + 1)
                nc.scalar.copy(qp[:, 1, :, :], qrest[:, :, :]).then_inc(q_mid, 1)
                wait(act, s_done, b)
                for nh in range(NB):
                    act.wait_ge(sums_done, 2 * b + nh + 1)
                    nc.scalar.copy(sT[:, nh * HALF:(nh + 1) * HALF], tp[nh][0:H, :]).then_inc(sums_taken, 1)

            over_batches(act, batch)
            shifts(B - 1)

        @block.tensor
        def _(pe):
            pe.wait_ge(weights, 16 * LOADS)
            pe.wait_ge(made, 2)

            def turn_sums(b):
                pe.wait_ge(sums_taken, 2 * b + 2)
                wait(pe, s_taken, b)
                pe.sem_inc(passed_pe, 1)
                for t in range(T):
                    last = nc.tensor.transpose(ps_s[:, t, :], sT[:, t * P:(t + 1) * P], ident[0:H, 0:H])
                last.then_inc(s_done, 1)

            def batch(b):
                def transposes(unit0, source):
                    for k in range(CH):
                        for half in range(NB):
                            u = unit0 + k * NB + half
                            if u >= 2:
                                pe.wait_ge(tp_taken, 8 * b + u - 1)
                            else:
                                wait(pe, tp_taken, 8 * b)
                            for i in range(4):
                                last = nc.tensor.transpose(tp[u % 2][:, i * P:(i + 1) * P], source(k, half * 4 + i),
                                                           ident[:, :])
                            last.then_inc(tp_done, 1)

                pe.wait_ge(xn_ready, b + 1)
                wait(pe, sums_taken, 2 * b)
                transposes(0, lambda k, t: xn[:, t, k * P:(k + 1) * P])
                if not isinstance(b, int):
                    turn_sums(b - 1)
                pe.wait_ge(tp_taken, 8 * b + 4)
                for which, w in ((0, wq), (1, wk)):
                    for g in range(CH):
                        for nh in range(NB):
                            u = 4 * which + g * NB + nh
                            if which == 0:
                                wait(pe, w_taken, 4 * b)
                            else:
                                pe.wait_ge(q_taken, 4 * b + g * NB + nh + 1)
                            for k in range(CH):
                                last = nc.tensor.matmul(pj[u % 4][:, :], w[:, k, g * P:(g + 1) * P],
                                                        xT[:, k, nh * HALF:(nh + 1) * HALF],
                                                        start=(k == 0), stop=(k == CH - 1))
                            last.then_inc(pj_done, 1)
                for i in range(4):
                    u = 8 + i
                    pe.wait_ge(k_taken, 4 * b + i + 1)
                    for t2 in range(2):
                        t = 2 * i + t2
                        for k in range(CH):
                            last = nc.tensor.matmul(pj[u % 4][:, t2 * D:(t2 + 1) * D], xT[:, k, t * P:(t + 1) * P],
                                                    wv[:, k, :], start=(k == 0), stop=(k == CH - 1))
                    last.then_inc(pj_done, 1)
                pe.wait_ge(k_centred, b + 1)
                transposes(4, lambda k, t: kT[:, k, t * P:(t + 1) * P])
                pe.wait_ge(tp_taken, 8 * b + 8)
                wait(pe, c_taken, b)
                for g in range(CH):
                    for t in range(T):
                        last = nc.tensor.matmul(ps_c[:, g, :], knat[:, t, g * P:(g + 1) * P],
                                                knat[:, t, g * P:(g + 1) * P], start=(t == 0), stop=(t == T - 1))
                last.then_inc(c_done, 1)
                pe.wait_ge(c_taken, b + 1)
                for g in range(CH):
                    for nh in range(NB):
                        u = 12 + g * NB + nh
                        pe.wait_ge(v_taken, 4 * b + g * NB + nh + 1)
                        nc.tensor.matmul(pj[u % 4][:, :], cm[:, g, :], qT[:, g, nh * HALF:(nh + 1) * HALF],
                                         start=True, stop=True).then_inc(pj_done, 1)
                pe.wait_ge(w_taken, 4 * b + 4)
                for nh in range(NB):
                    for g in range(CH):
                        last = nc.tensor.matmul(tp[nh][0:H, :], head_ones[:, g, :], prod[:, g, nh * HALF:(nh + 1) * HALF],
                                                start=(g == 0), stop=(g == CH - 1))
                    last.then_inc(sums_done, 1)

            over_batches(pe, batch)
            turn_sums(B - 1)


def attend(nc, qs, ks, vs, att):
    ctx = ExitStack()
    with ctx:
        def sb(name, shape, dt=F32):
            return ctx.enter_context(nc.sbuf_tensor(name, shape, dt))

        def pb(name, shape, dt=F32):
            return ctx.enter_context(nc.psum_tensor(name, shape, dt))

        def sem(name):
            return ctx.enter_context(nc.semaphore(name))

        def two(make, name, *a):
            return [make(f"{name}{i}", *a) for i in range(2)]

        ROWS = 2 * HD
        qa = two(sb, "qa", [P, N], BF16)
        qb = two(sb, "qb", [P, N], BF16)
        ka = two(sb, "ka", [P, N], BF16)
        kb = two(sb, "kb", [P, N], BF16)
        shift_in = two(sb, "shift_in", [P, T])
        qa2 = two(sb, "qa2_", [P, N], BF16)
        qb2 = two(sb, "qb2_", [P, N], BF16)
        ka2 = two(sb, "ka2_", [P, N], BF16)
        kb2 = two(sb, "kb2_", [P, N], BF16)
        zrow = two(sb, "zrow", [P, N], BF16)
        ones3 = sb("ones3", [P, P], BF16)
        v_in = two(sb, "v_in", [P, T * VW])
        Z = two(sb, "Z", [P, T, N])
        top = sb("top", [P, T])
        shift = two(sb, "shift", [P, T])
        peak = two(sb, "peak", [P, T])
        sign_out = two(sb, "sign_out", [P, N], BF16)
        acc = sb("acc", [P, T])
        tneg = two(sb, "tneg", [P, T])
        step = sb("step", [P, T])
        e_old, e_new, e_sq = sb("e_old", [P, T]), sb("e_new", [P, T]), sb("e_sq", [P, T])
        move, opposite, same = sb("move", [P, T]), sb("opposite", [P, T]), sb("same", [P, T])
        num, den = sb("num", [P, T]), sb("den", [P, T])
        above_keep, side, side_t = sb("above_keep", [P, T]), sb("side", [P, T]), sb("side_t", [P, T])
        t_side, minus_one = sb("t_side", [P, T]), sb("minus_one", [P, T])
        half_c = sb("half_c", [P, T])
        ge_out = [sb(f"ge_out{t}", [P, N], BF16) for t in range(T)]
        cnt = sb("cnt", [P, T])
        cnt_new = sb("cnt_new", [P, T])
        tC = sb("tC", [P, T])
        lo, hi = sb("lo", [P, T]), sb("hi", [P, T])
        err, miss, wide, tol = sb("err", [P, T]), sb("miss", [P, T]), sb("wide", [P, T]), sb("tol", [P, T])
        tnew, edge = sb("tnew", [P, T]), sb("edge", [P, T])
        pick = sb("pick", [P, T], I32)
        bad_col = sb("bad_col", [P, HD])
        bad_row = sb("bad_row", [P, HD])
        bad_int = sb("bad_int", [P, 1], I32)
        YRING = 4
        Y = [sb(f"Y{i}", [P, N]) for i in range(YRING)]
        cand = sb("cand", [P, T, 9])
        iota9 = sb("iota9", [P, T, 9])
        rank, sel = sb("rank", [P, T]), sb("sel", [P, T, 9])
        sel2 = sb("sel2", [P, T, 9])
        near = sb("near", [P, T])
        aug = sb("aug", [P, 2, T])
        aug_rest = sb("aug_rest", [P, 2, T])
        aug_parts = sb("aug_parts", [P, 2, PARTS, T], BF16)
        AUGW = 2 * PARTS * T
        identb = sb("identb", [P, P], BF16)
        augT = sb("augT", [AUGW, P], BF16)
        E = [sb(f"E{j}", [P, HALF]) for j in range(BY_MASK)]
        R = two(sb, "R", [P, HALF], BF16)
        minus_identb = sb("minus_identb", [P, P], BF16)
        minus_ones3 = sb("minus_ones3", [P, P], BF16)
        PR = two(sb, "PR", [P, HALF])
        oT = sb("oT", [VW, N])
        ident = sb("ident", [P, P])
        rden = sb("rden", [P, T])
        at = two(sb, "at", [P, T, HD])

        ps_s = two(pb, "ps_s", [P, N])
        DB = 3
        ps_d = [pb(f"ps_d{i}", [P, HALF]) for i in range(DB)]
        ps_m = pb("ps_m", [P, HALF])
        ps_v = ps_m[0:VW, :]
        ps_o = ps_m[:, 0:T * VW].rearrange("p (t w) -> p t w", w=VW)
        ps_t = ps_m[0:AUGW, T * VW:T * VW + P // 2].bitcast(BF16)

        made = sem("made")
        a_loaded = two(lambda n: sem(n), "a_loaded")
        d_loaded = two(lambda n: sem(n), "d_loaded")
        rows_loaded = two(lambda n: sem(n), "rows_loaded")
        s_done = sem("s_done")
        evac_done = sem("evac_done")
        counted = sem("counted")
        t_ready = sem("t_ready")
        passed_dve = sem("passed_dve")
        passed_pool = sem("passed_pool")
        passed_pe = sem("passed_pe")
        exact = sem("exact")
        sided = sem("sided")
        y_ready = sem("y_ready")
        sel_ready = sem("sel_ready")
        near_ready = sem("near_ready")
        flag_ready = sem("flag_ready")
        picked = sem("picked")
        ranked = sem("ranked")
        aug_ready = sem("aug_ready")
        augT_done = sem("augT_done")
        augT_copied = sem("augT_copied")
        d_done = sem("d_done")
        first_done = sem("first_done")
        second_done = sem("second_done")
        exp_done = sem("exp_done")
        mask_done = sem("mask_done")
        pv_done = sem("pv_done")
        half_copied = sem("half_copied")
        turned = sem("turned")
        at_ready = sem("at_ready")
        at_stored = two(lambda n: sem(n), "at_stored")

        LOADS = 8
        BLK = NB * T
        SCORES_AFTER = (6, 8, 9, 11, 12, 14)
        D_FROM = 7
        R1_FROM = 4
        FIRST = 4
        UPD = ROUNDS + 1

        block = ctx.enter_context(nc.Block())

        def run(engine, iteration):
            for k in range(-1, FIRST):
                iteration(k, k % 2)
            pairs = (GROUPS - 1 - FIRST) // 2
            with engine.Fori(0, pairs) as i:
                iteration(2 * i + FIRST, 0, True)
                iteration(2 * i + FIRST + 1, 1, True)
            for k in range(FIRST + 2 * pairs, GROUPS + 2):
                iteration(k, k % 2)

        def stages(k, steady):
            if steady:
                return True, True, True, True
            return tuple(0 <= g < GROUPS for g in (k + 1, k, k - 1, k - 2))

        def turn(k, par, off, n):
            if isinstance(k, int):
                return (k + off) // 2 * n
            return (k + off - (par + off) % 2) * (n // 2)

        SUMMED = tuple(j for j in range(BLK) if j not in MASKED)
        BY_SUM = len(SUMMED)

        def wait_product_operand(engine, g, j):
            if j in MASKED:
                engine.wait_ge(mask_done, BY_MASK * g + MASKED.index(j) + 1)
            else:
                engine.wait_ge(exp_done, BY_SUM * g + SUMMED.index(j) + 1)

        @block.sync
        def _(sp):
            def load(q_a, q_b, k_a, k_b, g, loaded):
                q, k = qs[g], ks[g]
                sp.dma_start(q_a[0:64, :], q[0:2]).then_inc(loaded, 16)
                sp.dma_start(q_a[64:128, :], q[0:2]).then_inc(loaded, 16)
                sp.dma_start(k_a[0:64, :], k[0:2]).then_inc(loaded, 16)
                sp.dma_start(k_a[64:96, :], k[1]).then_inc(loaded, 16)
                sp.dma_start(k_a[96:128, :], k[0]).then_inc(loaded, 16)
                sp.dma_start(q_b[0:64, :], q[0:3:2]).then_inc(loaded, 16)
                sp.dma_start(k_b[0:32, :], k[2]).then_inc(loaded, 16)
                sp.dma_start(k_b[32:64, :], k[0]).then_inc(loaded, 16)

            def load_a(g, par):
                load(qa[par], qb[par], ka[par], kb[par], g, a_loaded[par])
                sp.dma_start(shift_in[par][:, :], vs[g, :, T * VW:VROW]).then_inc(a_loaded[par], 16)

            def load_d(g, par):
                load(qa2[par], qb2[par], ka2[par], kb2[par], g, d_loaded[par])
                sp.dma_start(v_in[par][:, :], vs[g, :, 0:T * VW]).then_inc(d_loaded[par], 16)

            sp.wait_ge(made, 1)
            load_a(0, 0)

            def iteration(k, par, steady=False):
                do_a, do_b, do_c, do_d = stages(k, steady)
                if do_d:
                    sp.wait_ge(augT_copied, k - 1)
                    sp.dma_start(qb2[par][ROWS:ROWS + PARTS, :], augT[0:PARTS * T, :]).then_inc(rows_loaded[par], 16)
                    sp.dma_start(zrow[par][0:PARTS, :], augT[PARTS * T:AUGW, :]).then_inc(rows_loaded[par], 16)
                if steady or (0 <= k + 2 < GROUPS and k + 2 >= 1):
                    if steady or k >= 0:
                        sp.wait_ge(s_done, T * (k + 1))
                        sp.wait_ge(t_ready, UPD * k + 1)
                    load_a(k + 2, par)
                if do_c:
                    if steady or k - 3 >= 0:
                        sp.wait_ge(pv_done, BLK * (k - 2))
                    load_d(k - 1, 1 - par)
                if do_d:
                    sp.wait_ge(at_ready, k - 1)
                    sp.dma_start(att[k - 2].rearrange("(t p) d -> p t d", p=P), at[par][:, :, :]).then_inc(at_stored[par], 16)

            run(sp, iteration)
            for q in range(2):
                sp.wait_ge(at_stored[q], 16 * (GROUPS // 2))

        @block.gpsimd
        def _(pool):
            nc.gpsimd.memset(ident[:, :], 1.0)
            nc.gpsimd.memset(identb[:, :], 1.0)
            pool.drain()
            nc.gpsimd.affine_select(out=ident[:, :], in_=ident[:, :], compare_op=ALU.is_equal, fill=0.0, base=0,
                                    pattern=[[-1, P]], channel_multiplier=1)
            nc.gpsimd.affine_select(out=identb[:, :], in_=identb[:, :], compare_op=ALU.is_equal, fill=0.0, base=0,
                                    pattern=[[-1, P]], channel_multiplier=1)
            nc.gpsimd.memset(ones3[:, :], 1.0)
            nc.gpsimd.memset(minus_ones3[:, :], -1.0)
            pool.drain()
            nc.gpsimd.tensor_scalar(minus_identb[:, :], identb[:, :], -1.0, None, ALU.mult)
            nc.gpsimd.memset(half_c[:, :], float(KEEP))
            nc.gpsimd.memset(minus_one[:, :], -1.0)
            nc.gpsimd.memset(cand[:, :, 0:1], 0.0)
            for q in range(2):
                for x in (qb[q], kb[q], qb2[q], kb2[q]):
                    pool.drain()
                    nc.gpsimd.memset(x[ROWS:P, :], 0.0)
                pool.drain()
                nc.gpsimd.memset(zrow[q][:, :], 0.0)
                pool.drain()
                nc.gpsimd.memset(kb2[q][ROWS:ROWS + PARTS, :], 1.0)
            pool.drain()
            for i in range(9):
                nc.gpsimd.memset(iota9[:, :, i:i + 1], float(i))
            nc.gpsimd.memset(bad_col[:, :], 0.0)
            pool.drain().then_inc(made, 1)

            def ts(out, in0, s1, s2=None, op0=ALU.mult, op1=ALU.bypass):
                nc.gpsimd.tensor_scalar(out[:, :], in0[:, :], s1, s2, op0, op1)
                pool.drain()

            def tt(out, in0, in1, op):
                nc.gpsimd.tensor_tensor(out[:, :], in0[:, :], in1[:, :], op)
                pool.drain()

            def iteration(k, par, steady=False):
                do_a, do_b, do_c, do_d = stages(k, steady)
                old = 1 - par

                def read_count(r, e):
                    pool.wait_ge(counted, T * (ROUNDS * k + r + 1))
                    pool.sem_inc(passed_pool, 1)
                    ts(e, acc, 0.5, N / 2 - KEEP, ALU.mult, ALU.add)
                    tt(move, e, step, ALU.mult)

                def move_t(e):
                    tt(e_sq, e, e, ALU.mult)
                    ts(e_sq, e_sq, WINDOW, None, ALU.is_gt)
                    tt(move, move, e_sq, ALU.mult)
                    nc.gpsimd.tensor_tensor(tneg[par][:, :], tneg[par][:, :], move[:, :], ALU.subtract)
                    pool.drain().then_inc(t_ready, 1)

                def distances(t):
                    n = T * (k - 1) + t
                    if steady or n >= YRING:
                        pool.wait_ge(ranked, n - YRING + 1)
                    pool.sem_inc(passed_pool, 1)
                    nc.gpsimd.tensor_scalar(Y[t % YRING][:, :], Z[old][:, t, :], side[:, t:t + 1], side_t[:, t:t + 1],
                                            ALU.mult, ALU.add).then_inc(y_ready, 1)

                def begin(q):
                    pool.wait_ge(evac_done, T * (k + 2))
                    pool.sem_inc(passed_pool, 1)
                    nc.gpsimd.tensor_scalar(shift[q][:, :], shift_in[q][:, :], 1.0, None, ALU.mult)
                    nc.gpsimd.tensor_scalar(peak[q][:, :], top[:, :], 1.0, None, ALU.mult)
                    nc.gpsimd.tensor_scalar(step[:, :], shift_in[q][:, :], SPACING, None, ALU.mult)
                    nc.gpsimd.tensor_scalar(tneg[q][:, :], shift_in[q][:, :], -1.0, None, ALU.mult)
                    pool.drain().then_inc(t_ready, 1)

                if do_b:
                    read_count(0, e_old)
                    move_t(e_old)
                if do_c:
                    pool.wait_ge(flag_ready, k)
                    pool.sem_inc(passed_pool, 1)
                    ts(above_keep, cnt, float(KEEP), None, ALU.is_gt)
                    ts(side, above_keep, -2.0, 1.0, ALU.mult, ALU.add)
                    ts(t_side, tC, BELOW)
                    tt(side_t, tC, t_side, ALU.subtract)
                    tt(side_t, side_t, above_keep, ALU.mult)
                    tt(t_side, t_side, side_t, ALU.add)
                    tt(side_t, t_side, side, ALU.mult)
                    ts(side_t, side_t, -1.0)
                    for t in range(T):
                        if t == YRING:
                            pool.wait_ge(exact, k)
                        distances(t)
                    ts(rank, cnt, -1.0, float(KEEP), ALU.mult, ALU.add)
                    tt(rank, rank, side, ALU.mult)
                    if steady or k >= 2:
                        pool.wait_ge(near_ready, k - 1)
                    nc.gpsimd.tensor_tensor(sel[:, :, :], iota9[:, :, :], rank[:, :].unsqueeze(2).broadcast_to([P, T, 9]),
                                            ALU.subtract)
                    pool.drain()
                    nc.gpsimd.tensor_scalar(sel2[:, :, :], sel[:, :, :], -0.5, None, ALU.add)
                    pool.drain()
                    nc.gpsimd.tensor_tensor(sel[:, :, :], sel2[:, :, :], sel2[:, :, :], ALU.mult)
                    pool.drain()
                    nc.gpsimd.tensor_scalar(sel2[:, :, :], sel[:, :, :], 0.25, 0.5, ALU.is_equal, ALU.mult)
                    pool.drain().then_inc(sel_ready, 1)
                    nc.gpsimd.tensor_tensor(aug[:, 0, :], shift[old][:, :], peak[old][:, :], ALU.subtract)
                    nc.gpsimd.tensor_scalar(aug[:, 1, :], peak[old][:, :], 1.0 + TINY, None, ALU.mult)
                    pool.drain()
                if do_b:
                    read_count(1, e_new)
                    tt(opposite, e_old, e_new, ALU.mult)
                    ts(opposite, opposite, 0.0, None, ALU.is_lt)
                    ts(same, opposite, -CAUTION, CAUTION, ALU.mult, ALU.add)
                    tt(num, e_old, opposite, ALU.mult)
                    tt(den, e_new, opposite, ALU.mult)
                    tt(num, num, same, ALU.add)
                    tt(den, num, den, ALU.subtract)
                    tt(num, num, den, ALU.mult)
                    tt(den, den, den, ALU.mult)
                    tt(den, den, minus_one, ALU.pow)
                    tt(num, num, den, ALU.mult)
                    tt(move, move, num, ALU.mult)
                    move_t(e_new)
                if do_a:
                    begin(old)
                if do_c:
                    pool.wait_ge(near_ready, k)
                    pool.sem_inc(passed_pool, 1)
                    tt(near, near, side, ALU.mult)
                    tt(near, near, t_side, ALU.add)
                    nc.gpsimd.tensor_tensor(aug[:, 1, :], aug[:, 1, :], near[:, :], ALU.subtract)
                    pool.drain()
                    if steady or k >= 2:
                        pool.wait_ge(augT_done, k - 1)
                    pool.sem_inc(passed_pool, 1)
                    nc.gpsimd.tensor_copy(aug_parts[:, :, 0, :], aug[:, :, :])
                    pool.drain()
                    nc.gpsimd.tensor_tensor(aug_rest[:, :, :], aug[:, :, :], aug_parts[:, :, 0, :], ALU.subtract)
                    pool.drain()
                    nc.gpsimd.tensor_copy(aug_parts[:, :, 1, :], aug_rest[:, :, :])
                    pool.drain()
                    nc.gpsimd.tensor_tensor(aug_parts[:, :, 2, :], aug_rest[:, :, :], aug_parts[:, :, 1, :], ALU.subtract)
                    pool.drain().then_inc(aug_ready, 1)

            run(pool, iteration)

        @block.scalar
        def _(act):
            def iteration(k, par, steady=False):
                do_a, do_b, do_c, do_d = stages(k, steady)
                g = k - 2

                def count(r, t):
                    if t == 0:
                        act.wait_ge(t_ready, UPD * k + r + 1)
                    n = T * r + t
                    if steady or k > 0 or n >= 2:
                        act.wait_ge(counted, ROUNDS * T * k + n - 1)
                    nc.scalar.activation(sign_out[n % 2][:, :], Z[par][:, t, :], ACT.Sign, bias=tneg[par][:, t:t + 1],
                                         accum_out=acc[:, t:t + 1]).then_inc(counted, 1)

                def first(j):
                    act.wait_ge(d_done, BLK * g + j + 1)
                    if j in MASKED:
                        m = MASKED.index(j)
                        if steady or k > 2:
                            act.wait_ge(mask_done, BY_MASK * (g - 1) + m + 1)
                        nc.scalar.activation(E[m][:, :], ps_d[j % DB][:, :], ACT.Exp,
                                             scale=SCALE).then_inc(first_done, 1)
                    else:
                        if steady or k > 2 or j >= 2:
                            act.wait_ge(second_done, BLK * g + j - 1)
                        nc.scalar.activation(R[j % 2][:, :], ps_d[j % DB][:, :], ACT.Relu,
                                             scale=-FAR).then_inc(first_done, 1)

                def exponent(j):
                    act.wait_ge(second_done, BLK * g + j + 1)
                    if steady or k > 2 or j >= 2:
                        act.wait_ge(pv_done, BLK * g + j - 1)
                    nc.scalar.activation(PR[j % 2][:, :], ps_d[j % DB][:, :], ACT.Exp, scale=SCALE).then_inc(exp_done, 1)

                def copy_half(nh):
                    act.wait_ge(pv_done, BLK * g + T * (nh + 1))
                    if nh == 0 and (steady or k > 2):
                        act.wait_ge(turned, k - 2)
                    nc.scalar.copy(oT[:, nh * HALF:(nh + 1) * HALF], ps_v).then_inc(half_copied, 1)

                def block_of_d(j):
                    if j + 1 < BLK:
                        first(j + 1)
                    if j in SUMMED:
                        exponent(j)
                    if j == T:
                        copy_half(0)

                for t in range(T):
                    if do_b:
                        count(0, t)
                    if do_d and t == 1:
                        act.wait_ge(augT_done, k - 1)
                        if steady or k >= 3:
                            act.wait_ge(rows_loaded[1 - par], turn(k, par, -3, 32) + 32)
                        nc.scalar.copy(augT[:, :], ps_t).then_inc(augT_copied, 1)
                    if do_d and t == D_FROM - 1:
                        first(0)
                    if do_d and t >= D_FROM:
                        block_of_d(t - D_FROM)
                for j in range(T - D_FROM, BLK):
                    if do_d:
                        block_of_d(j)
                    if do_b and 0 <= j - R1_FROM < T:
                        count(1, j - R1_FROM)
                if do_d:
                    copy_half(1)

            run(act, iteration)

        @block.vector
        def _(dve):
            dve.wait_ge(made, 1)
            regs = [dve.alloc_register(f"bad_q{q}") for q in range(4)]
            bad = dve.alloc_register("bad")

            def iteration(k, par, steady=False):
                do_a, do_b, do_c, do_d = stages(k, steady)
                old = 1 - par

                def load_flag():
                    for q in range(4):
                        dve.load(regs[q], bad_int[HD * q:HD * q + 1, 0:1])
                    dve.reg_mov(bad, dve.snap(regs[0]) + dve.snap(regs[1]) + dve.snap(regs[2]) + dve.snap(regs[3]))

                def reduce_flag():
                    nc.vector.reduce_max(bad_col[:, 0:1], miss[:, :], AX_X)
                    dve.drain()
                    nc.vector.transpose(bad_row[:, :], bad_col[:, :])
                    dve.drain()
                    return nc.vector.reduce_max(bad_int[:, :], bad_row[:, :], AX_X)

                def exact_counts(at, count):
                    for t in range(T):
                        nc.vector.tensor_scalar(ge_out[t][:, :], Z[old][:, t, :], at[:, t:t + 1], None, ALU.is_ge, ALU.add,
                                                accum_out=count[:, t:t + 1])
                    dve.drain()

                def judge():
                    nc.vector.tensor_scalar(err[:, :], cnt[:, :], -float(KEEP), None, ALU.add)
                    dve.drain()
                    nc.vector.tensor_tensor(miss[:, :], err[:, :], err[:, :], ALU.mult)
                    dve.drain()
                    nc.vector.tensor_scalar(miss[:, :], miss[:, :], WINDOW, None, ALU.is_gt)
                    dve.drain()

                def narrow():
                    nc.vector.tensor_scalar(pick[:, :], cnt[:, :], float(KEEP + REACH), None, ALU.is_gt)
                    dve.drain()
                    nc.vector.copy_predicated(lo[:, :], pick[:, :], tC[:, :])
                    dve.drain()
                    nc.vector.tensor_scalar(pick[:, :], cnt[:, :], float(KEEP - REACH), None, ALU.is_lt)
                    dve.drain()
                    nc.vector.copy_predicated(hi[:, :], pick[:, :], tC[:, :])
                    dve.drain()
                    nc.vector.tensor_tensor(wide[:, :], hi[:, :], lo[:, :], ALU.subtract)
                    dve.drain()

                def settle():
                    nc.vector.tensor_tensor(tnew[:, :], wide[:, :], tol[:, :], ALU.is_le)
                    dve.drain()
                    nc.vector.tensor_tensor(pick[:, :], tnew[:, :], miss[:, :], ALU.mult)
                    dve.drain()
                    nc.vector.copy_predicated(tC[:, :], pick[:, :], lo[:, :])
                    nc.vector.copy_predicated(cnt[:, :], pick[:, :], half_c[:, :])
                    dve.drain()
                    nc.vector.tensor_tensor(tnew[:, :], wide[:, :], tol[:, :], ALU.is_gt)
                    dve.drain()
                    nc.vector.tensor_tensor(miss[:, :], miss[:, :], tnew[:, :], ALU.mult)
                    dve.drain()

                def mend():
                    nc.vector.tensor_scalar(above_keep[:, :], cnt[:, :], float(KEEP), None, ALU.is_gt)
                    nc.vector.tensor_scalar(t_side[:, :], tC[:, :], BELOW, None, ALU.mult)
                    dve.drain()
                    nc.vector.tensor_scalar(side[:, :], above_keep[:, :], -2.0, 1.0, ALU.mult, ALU.add)
                    nc.vector.tensor_tensor(side_t[:, :], tC[:, :], t_side[:, :], ALU.subtract)
                    dve.drain()
                    nc.vector.tensor_tensor(side_t[:, :], side_t[:, :], above_keep[:, :], ALU.mult)
                    dve.drain()
                    nc.vector.tensor_tensor(t_side[:, :], t_side[:, :], side_t[:, :], ALU.add)
                    dve.drain()
                    nc.vector.tensor_tensor(side_t[:, :], t_side[:, :], side[:, :], ALU.mult)
                    dve.drain()
                    nc.vector.tensor_scalar(side_t[:, :], side_t[:, :], -1.0, None, ALU.mult)
                    dve.drain()
                    for t in range(YRING):
                        nc.vector.tensor_scalar(Y[t][:, :], Z[old][:, t, :], side[:, t:t + 1], side_t[:, t:t + 1],
                                                ALU.mult, ALU.add)
                    dve.drain()

                def search(newton):
                    if newton:
                        nc.vector.tensor_tensor(tnew[:, :], err[:, :], shift[old][:, :], ALU.mult)
                        dve.drain()
                        nc.vector.scalar_tensor_tensor(tnew[:, :], tnew[:, :], 0.5 * SPACING, tC[:, :], ALU.mult, ALU.add)
                        nc.vector.scalar_tensor_tensor(edge[:, :], wide[:, :], MARGIN, lo[:, :], ALU.mult, ALU.add)
                        dve.drain()
                        nc.vector.tensor_tensor(tnew[:, :], tnew[:, :], edge[:, :], ALU.max)
                        dve.drain()
                        nc.vector.scalar_tensor_tensor(edge[:, :], wide[:, :], 1.0 - MARGIN, lo[:, :], ALU.mult, ALU.add)
                        dve.drain()
                        nc.vector.tensor_tensor(tnew[:, :], tnew[:, :], edge[:, :], ALU.min)
                    else:
                        nc.vector.scalar_tensor_tensor(tnew[:, :], wide[:, :], 0.5, lo[:, :], ALU.mult, ALU.add)
                    nc.vector.tensor_copy(pick[:, :], miss[:, :])
                    dve.drain()
                    nc.vector.copy_predicated(tC[:, :], pick[:, :], tnew[:, :])
                    dve.drain()
                    exact_counts(tC, cnt)
                    judge()
                    narrow()
                    settle()
                    reduce_flag()
                    dve.drain()
                    load_flag()

                def mask(j):
                    dve.wait_ge(second_done, BLK * (k - 2) + j + 1)
                    if steady or k > 2 or j >= 2:
                        dve.wait_ge(pv_done, BLK * (k - 2) + j - 1)
                    nc.vector.scalar_tensor_tensor(PR[j % 2][:, :], ps_d[j % DB][:, :], 0.0, E[MASKED.index(j)][:, :],
                                                   ALU.is_ge, ALU.mult).then_inc(mask_done, 1)

                if do_c:
                    dve.wait_ge(t_ready, UPD * k)
                    nc.vector.tensor_scalar(tC[:, :], tneg[old][:, :], -1.0, None, ALU.mult)
                    dve.drain()
                    exact_counts(tC, cnt)
                    judge()
                    reduce_flag().then_inc(flag_ready, 1)
                if do_d:
                    for j in MASKED[:2]:
                        mask(j)
                if do_c:
                    dve.wait_ge(flag_ready, k)
                    dve.sem_inc(passed_dve, 1)
                    load_flag()
                    with dve.If(dve.snap(bad) > 0):
                        dve.drain()
                        nc.vector.tensor_tensor(tnew[:, :], err[:, :], shift[old][:, :], ALU.mult)
                        dve.drain()
                        nc.vector.tensor_tensor(tnew[:, :], tnew[:, :], miss[:, :], ALU.mult)
                        dve.drain()
                        nc.vector.scalar_tensor_tensor(tnew[:, :], tnew[:, :], 0.5 * SPACING, tC[:, :], ALU.mult, ALU.add)
                        dve.drain()
                        exact_counts(tnew, cnt_new)
                        dve.wait_ge(y_ready, T * (k - 1) + YRING)
                        dve.sem_inc(passed_dve, 1)
                        nc.vector.tensor_scalar(tC[:, :], tnew[:, :], 1.0, None, ALU.mult)
                        nc.vector.tensor_scalar(cnt[:, :], cnt_new[:, :], 1.0, None, ALU.mult)
                        dve.drain()
                        judge()
                        reduce_flag()
                        dve.drain()
                        load_flag()
                        with dve.If(dve.snap(bad) > 0):
                            nc.vector.tensor_scalar(lo[:, :], shift[old][:, :], 0.25, None, ALU.mult)
                            nc.vector.tensor_scalar(hi[:, :], shift[old][:, :], 1.75, None, ALU.mult)
                            nc.vector.tensor_scalar(tol[:, :], shift[old][:, :], TINY, None, ALU.mult)
                            dve.drain()
                            narrow()
                            with dve.While(lambda: dve.snap(bad) > 0):
                                search(True)
                                with dve.If(dve.snap(bad) > 0):
                                    search(True)
                                    with dve.If(dve.snap(bad) > 0):
                                        search(False)
                        mend()
                    dve.sem_inc(exact, 1)
                if do_d:
                    mask(MASKED[2])
                for t in range(T):
                    if do_c:
                        dve.wait_ge(y_ready, T * (k - 1) + t + 1)
                        y = Y[t % YRING]
                        nc.vector.scalar_tensor_tensor(y[:, :], y[:, :], -FAR, y[:, :], ALU.mult, ALU.min).then_inc(picked, 1)
                    if do_a:
                        dve.wait_ge(s_done, T * (k + 1) + t + 1)
                        if t == 0:
                            dve.wait_ge(a_loaded[old], turn(k, par, 1, 16 * (LOADS + 1)) + 16 * (LOADS + 1))
                            if steady or k >= 0:
                                dve.wait_ge(t_ready, UPD * k + 1)
                        nc.vector.tensor_scalar(Z[old][:, t, :], ps_s[t % 2][:, :], shift_in[old][:, t:t + 1], None,
                                                ALU.add, ALU.max, accum_out=top[:, t:t + 1]).then_inc(evac_done, 1)
                    if do_c:
                        dve.wait_ge(picked, T * (k - 1) + t + 1)
                        dve.sem_inc(passed_dve, 1)
                        nc.vector.max(cand[:, t, 1:9], Y[t % YRING][:, :]).then_inc(ranked, 1)
                    if do_d and t < BY_MASK - 3:
                        mask(MASKED[3 + t])
                if do_c:
                    dve.wait_ge(sel_ready, k)
                    dve.wait_ge(ranked, T * k)
                    nc.vector.tensor_tensor(sel[:, :, :], sel2[:, :, :], cand[:, :, :], ALU.mult)
                    dve.drain()
                    nc.vector.reduce_sum(near[:, :], sel[:, :, :], AX_X).then_inc(near_ready, 1)
                if do_d:
                    dve.wait_ge(turned, k - 1)
                    if steady or k - 4 >= 0:
                        dve.wait_ge(at_stored[par], turn(k, par, -2, 16))
                    nc.vector.reciprocal(rden[:, :], ps_o[:, :, HD])
                    dve.drain()
                    nc.vector.tensor_tensor(at[par][:, :, :], ps_o[:, :, 0:HD],
                                            rden[:, :].unsqueeze(2).broadcast_to([P, T, HD]), ALU.mult).then_inc(at_ready, 1)

            run(dve, iteration)

        @block.tensor
        def _(pe):
            pe.wait_ge(made, 1)

            def iteration(k, par, steady=False):
                do_a, do_b, do_c, do_d = stages(k, steady)
                new = 1 - par
                g = k - 2

                def scores(t):
                    if t == 0:
                        pe.wait_ge(a_loaded[new], turn(k, par, 1, 16 * (LOADS + 1)) + 16 * (LOADS + 1))
                    if steady or k >= 0 or t >= 2:
                        pe.wait_ge(evac_done, T * (k + 1) + t - 1)
                    for h in range(NB):
                        s = slice(h * HALF, (h + 1) * HALF)
                        nc.tensor.matmul(ps_s[t % 2][:, s], qa[new][:, t * P:(t + 1) * P], ka[new][:, s],
                                         start=True, stop=False)
                        last = nc.tensor.matmul(ps_s[t % 2][:, s], qb[new][:, t * P:(t + 1) * P], kb[new][:, s],
                                                start=False, stop=True)
                    last.then_inc(s_done, 1)

                def distance(j):
                    nh, t = j // T, j % T
                    s = slice(nh * HALF, (nh + 1) * HALF)
                    if j == 0:
                        pe.wait_ge(d_loaded[par], turn(k, par, -2, 16 * (LOADS + 1)) + 16 * (LOADS + 1))
                        pe.wait_ge(rows_loaded[par], turn(k, par, -2, 32) + 32)
                    if j >= DB:
                        wait_product_operand(pe, g, j - DB)
                    elif j == 0 and (steady or k > 2):
                        wait_product_operand(pe, g - 1, BLK - 1)
                    nc.tensor.matmul(ps_d[j % DB][:, :], ka2[par][:, t * P:(t + 1) * P], qa2[par][:, s],
                                     start=True, stop=False)
                    last = nc.tensor.matmul(ps_d[j % DB][:, :], kb2[par][:, t * P:(t + 1) * P], qb2[par][:, s],
                                            start=False, stop=(j in MASKED))
                    if j in SUMMED:
                        last = nc.tensor.matmul(ps_d[j % DB][:, :], ones3[:, :], zrow[par][:, s],
                                                start=False, stop=True)
                    last.then_inc(d_done, 1)

                def second(j):
                    s = slice(j // T * HALF, (j // T + 1) * HALF)
                    pe.wait_ge(first_done, BLK * g + j + 1)
                    if j in MASKED:
                        last = nc.tensor.matmul(ps_d[j % DB][:, :], ones3[:, :], zrow[par][:, s],
                                                start=False, stop=True, skip_group_check=True)
                    else:
                        nc.tensor.matmul(ps_d[j % DB][:, :], minus_ones3[:, :], zrow[par][:, s],
                                         start=False, stop=False, skip_group_check=True)
                        last = nc.tensor.matmul(ps_d[j % DB][:, :], minus_identb[:, :], R[j % 2][:, :],
                                                start=False, stop=True, skip_group_check=True)
                    last.then_inc(second_done, 1)

                def product(j):
                    nh, t = j // T, j % T
                    wait_product_operand(pe, g, j)
                    if j == T:
                        pe.wait_ge(half_copied, NB * g + 1)
                    nc.tensor.matmul(ps_v, v_in[par][:, t * VW:(t + 1) * VW], PR[j % 2][:, :],
                                     start=(t == 0), stop=(t == T - 1)).then_inc(pv_done, 1)

                if do_a:
                    scores(0)
                    scores(1)
                if do_d:
                    pe.wait_ge(aug_ready, k - 1)
                    if steady or k >= 3:
                        pe.wait_ge(at_ready, k - 2)
                        pe.wait_ge(augT_copied, k - 2)
                    pe.sem_inc(passed_pe, 1)
                    nc.tensor.transpose(ps_t, aug_parts[:, :, :, :].rearrange("p a i t -> p (a i t)"),
                                        identb[:, :]).then_inc(augT_done, 1)
                    for j in range(DB):
                        distance(j)
                for j in range(BLK):
                    if do_d:
                        second(j)
                        if j >= 1:
                            if j + 2 < BLK:
                                distance(j + 2)
                            product(j - 1)
                    if do_a and j in SCORES_AFTER:
                        scores(SCORES_AFTER.index(j) + 2)
                if do_d:
                    product(BLK - 1)
                    pe.wait_ge(half_copied, NB * g + NB)
                    pe.sem_inc(passed_pe, 1)
                    for t in range(T):
                        last = nc.tensor.transpose(ps_o[:, t, :], oT[:, t * P:(t + 1) * P], ident[0:VW, 0:VW])
                    last.then_inc(turned, 1)

            run(pe, iteration)


def finish(nc, x, att, Wo, bo, W_r, W_k, W_v, mu_r, mu_k, out):
    ctx = ExitStack()
    with ctx:
        def sb(name, shape, dt=F32):
            return ctx.enter_context(nc.sbuf_tensor(name, shape, dt))

        def sem(name):
            return ctx.enter_context(nc.semaphore(name))

        ident = sb("f_ident", [P, P])
        wo = sb("f_wo", [P, CH, D])
        w_in = [sb(f"f_w_in{i}", [P, CH, D]) for i in range(3)]
        wT = [sb(f"f_wT{i}", [P, CH, D]) for i in range(3)]
        bo_row = sb("f_bo", [P, D])
        mu = [sb(f"f_mu{i}", [P, CH]) for i in range(2)]
        omu = [sb(f"f_omu{i}", [P, CH]) for i in range(2)]
        exps = sb("f_exps", [P, T])
        x_in = sb("f_x", [P, T, D])
        a_in = sb("f_a", [P, T, D])
        aT = sb("f_aT", [P, CH, N])
        x2 = sb("f_x2", [P, T, D])
        x2_kept = sb("f_x2_kept", [P, T, D])
        bst = sb("f_bst", [P, T, 6])
        mv = sb("f_mv", [P, T, 2])
        var_eps = sb("f_var", [P, T])
        rstd = sb("f_rstd", [P, T])
        xn = sb("f_xn", [P, T, D])
        hT = sb("f_hT", [P, CH, N + 2])
        prev = [sb(f"f_prev{i}", [P, CH, N]) for i in range(2)]
        mix = [sb(f"f_mix{i}", [P, CH, N]) for i in range(2)]
        kact = sb("f_kact", [P, CH, N])
        gate = sb("f_gate", [P, T, D])
        res = sb("f_res", [P, T, D])

        tp = [ctx.enter_context(nc.psum_tensor(f"f_tp{i}", [P, HALF], F32)) for i in range(2)]
        pj = [ctx.enter_context(nc.psum_tensor(f"f_pj{i}", [P, HALF], F32)) for i in range(4)]

        weights = sem("f_weights")
        made = sem("f_made")
        wt_done = sem("f_wt_done")
        wt_taken = sem("f_wt_taken")
        omu_ready = sem("f_omu_ready")
        x_loaded = sem("f_x_loaded")
        a_loaded = sem("f_a_loaded")
        x_biased = sem("f_x_biased")
        a_turned = sem("f_a_turned")
        a_copied = sem("f_a_copied")
        x_turned = sem("f_x_turned")
        x_copied = sem("f_x_copied")
        wo_done = sem("f_wo_done")
        k_done = sem("f_k_done")
        r_done = sem("f_r_done")
        v_done = sem("f_v_done")
        kept = sem("f_kept")
        y_taken = sem("f_y_taken")
        stats = sem("f_stats")
        rstd_ready = sem("f_rstd_ready")
        xn_ready = sem("f_xn_ready")
        prev_ready = sem("f_prev_ready")
        mix_ready = sem("f_mix_ready")
        relu_done = sem("f_relu_done")
        k_taken = sem("f_k_taken")
        gate_ready = sem("f_gate_ready")
        v_taken = sem("f_v_taken")
        res_ready = sem("f_res_ready")
        stored = sem("f_stored")
        LOADS = 7
        block = ctx.enter_context(nc.Block())

        @block.sync
        def _(sp):
            sp.dma_start(wo[:, :, :], Wo.rearrange("(k p) d -> p k d", p=P)).then_inc(weights, 16)
            for w, src in zip(w_in, (W_r, W_k, W_v)):
                sp.dma_start(w[:, :, :], src.rearrange("(k p) d -> p k d", p=P)).then_inc(weights, 16)
            sp.dma_start(bo_row[:, :], bo.partition_broadcast(P)).then_inc(weights, 16)
            for m, src in zip(mu, (mu_r, mu_k)):
                sp.dma_start(m[:, :], src.rearrange("(k p) -> p k", p=P),
                             allow_slow_non_contiguous=True).then_inc(weights, 16)

            def load(b):
                wait(sp, a_turned, 4 * b)
                wait(sp, y_taken, 4 * b)
                for h in range(H):
                    sp.dma_start(a_in[:, :, h * HD:(h + 1) * HD],
                                 att[b, h].rearrange("(t p) d -> p t d", p=P)).then_inc(a_loaded, 16)
                sp.dma_start(x_in[:, :, :], x[b].rearrange("(t p) d -> p t d", p=P)).then_inc(x_loaded, 16)

            def store(b):
                sp.wait_ge(res_ready, b + 1)
                sp.dma_start(out[b].rearrange("(t p) d -> p t d", p=P), res[:, :, :]).then_inc(stored, 16)

            load(0)
            load(1)
            with sp.Fori(2, B) as b:
                load(b)
                store(b - 2)
            store(B - 2)
            store(B - 1)
            sp.wait_ge(stored, 16 * B)

        @block.gpsimd
        def _(pool):
            make_identity(pool, nc, ident, made)
            nc.gpsimd.memset(exps[:, :], -0.5)
            nc.gpsimd.memset(hT[:, :, 1:2], 0.0)
            pool.drain().then_inc(made, 1)
            pool.wait_ge(weights, 16 * LOADS)

            def residual_bias(b):
                pool.wait_ge(x_loaded, 16 * b + 16)
                for t in range(T):
                    nc.gpsimd.tensor_tensor(x_in[:, t, :], x_in[:, t, :], bo_row[:, :], ALU.add)
                pool.drain().then_inc(x_biased, 1)

            def inverse_root(b):
                pool.wait_ge(stats, b + 1)
                nc.gpsimd.tensor_tensor(rstd[:, :], var_eps[:, :], exps[:, :], ALU.pow).then_inc(rstd_ready, 1)

            def batch(b, more=True):
                if more:
                    residual_bias(b + 1)
                    inverse_root(b + 1)

            residual_bias(0)
            inverse_root(0)
            over_batches(pool, batch, ahead=True)

        @block.vector
        def _(dve):
            dve.wait_ge(weights, 16 * LOADS)
            dve.wait_ge(made, 2)
            for i in range(2):
                nc.vector.tensor_scalar(omu[i][:, :], mu[i][:, :], -1.0, 1.0, ALU.mult, ALU.add)
            dve.drain().then_inc(omu_ready, 1)

            def residual(b):
                dve.wait_ge(x_biased, b + 1)
                wait(dve, kept, b)
                for u in range(4):
                    dve.wait_ge(wo_done, 4 * b + u + 1)
                    nc.vector.tensor_tensor(x2[:, 2 * u:2 * u + 2, :], x_in[:, 2 * u:2 * u + 2, :],
                                            pj[u][:, :].rearrange("p (t d) -> p t d", t=2), ALU.add).then_inc(y_taken, 1)
                dve.drain()
                for t in range(T):
                    nc.vector.bn_stats(bst[:, t, :], x2[:, t, :])
                dve.drain()
                for t in range(T):
                    nc.vector.bn_aggr(mv[:, t, :], bst[:, t, :])
                dve.drain()
                nc.vector.tensor_scalar(var_eps[:, :], mv[:, :, 1], EPS, None, ALU.add).then_inc(stats, 1)

            def normalise(b):
                dve.wait_ge(rstd_ready, b + 1)
                wait(dve, x_turned, 4 * b)
                for t in range(T):
                    last = nc.vector.tensor_scalar(xn[:, t, :], x2[:, t, :], mv[:, t, 0:1], rstd[:, t:t + 1],
                                                   ALU.subtract, ALU.mult)
                last.then_inc(xn_ready, 1)

            def batch(b, more=True):
                for i in (1, 0):
                    dve.wait_ge(prev_ready, 2 * b + 2 - i)
                    for k in range(CH):
                        last = nc.vector.scalar_tensor_tensor(mix[i][:, k, :], hT[:, k, 2:N + 2], mu[i][:, k:k + 1],
                                                              prev[i][:, k, :], ALU.mult, ALU.add)
                    last.then_inc(mix_ready, 1)
                if more:
                    residual(b + 1)
                for g in range(CH):
                    for nh in range(NB):
                        u = g * NB + nh
                        s = slice(nh * HALF, (nh + 1) * HALF)
                        dve.wait_ge(relu_done, 4 * b + u + 1)
                        nc.vector.tensor_tensor(kact[:, g, s], kact[:, g, s], pj[u][:, :], ALU.mult).then_inc(k_taken, 1)
                if more:
                    normalise(b + 1)
                wait(dve, stored, 16 * b)
                for i in range(4):
                    s = slice(2 * i, 2 * i + 2)
                    dve.wait_ge(gate_ready, 4 * b + i + 1)
                    dve.wait_ge(v_done, 4 * b + i + 1)
                    nc.vector.tensor_tensor(res[:, s, :], gate[:, s, :], pj[i][:, :].rearrange("p (t d) -> p t d", t=2),
                                            ALU.mult).then_inc(v_taken, 1)
                dve.drain()
                dve.wait_ge(kept, b + 1)
                nc.vector.tensor_tensor(res[:, :, :], res[:, :, :], x2_kept[:, :, :], ALU.add).then_inc(res_ready, 1)

            residual(0)
            normalise(0)
            over_batches(dve, batch, ahead=True)

        @block.scalar
        def _(act):
            act.wait_ge(omu_ready, 1)
            for i in range(3):
                act.wait_ge(wt_done, i + 1)
                nc.scalar.copy(wT[i][:, :, :], tp[i % 2][:, :].rearrange("p (k d) -> p k d", k=CH)).then_inc(wt_taken, 1)

            def attention_rows(b):
                wait(act, wo_done, 4 * b)
                for k in range(CH):
                    for half in range(NB):
                        u = k * NB + half
                        act.wait_ge(a_turned, 4 * b + u + 1)
                        nc.scalar.copy(aT[:, k, half * HALF:(half + 1) * HALF], tp[u % 2][:, :]).then_inc(a_copied, 1)

            def batch(b, more=True):
                wait(act, mix_ready, 2 * b)
                for k in range(CH):
                    for half in range(NB):
                        u = k * NB + half
                        act.wait_ge(x_turned, 4 * b + u + 1)
                        nc.scalar.copy(hT[:, k, 2 + half * HALF:2 + (half + 1) * HALF], tp[u % 2][:, :]).then_inc(x_copied, 1)
                if more:
                    attention_rows(b + 1)
                act.wait_ge(y_taken, 4 * b + 4)
                wait(act, res_ready, b)
                nc.scalar.copy(x2_kept[:, :, :], x2[:, :, :]).then_inc(kept, 1)
                act.wait_ge(x_copied, 4 * b + 4)
                for i in (1, 0):
                    for k in range(CH):
                        last = nc.scalar.activation(prev[i][:, k, :], hT[:, k, 1:N + 1], ACT.Identity,
                                                    scale=omu[i][:, k:k + 1])
                    last.then_inc(prev_ready, 1)
                wait(act, v_done, 4 * b)
                for g in range(CH):
                    for nh in range(NB):
                        u = g * NB + nh
                        act.wait_ge(k_done, 4 * b + u + 1)
                        nc.scalar.activation(kact[:, g, nh * HALF:(nh + 1) * HALF], pj[u][:, :], ACT.Relu).then_inc(relu_done, 1)
                for i in range(4):
                    act.wait_ge(r_done, 4 * b + i + 1)
                    nc.scalar.activation(gate[:, 2 * i:2 * i + 2, :], pj[i][:, :].rearrange("p (t d) -> p t d", t=2),
                                         ACT.Sigmoid).then_inc(gate_ready, 1)

            attention_rows(0)
            over_batches(act, batch, ahead=True)

        @block.tensor
        def _(pe):
            pe.wait_ge(weights, 16 * LOADS)
            pe.wait_ge(made, 2)
            for i in range(3):
                if i == 2:
                    pe.wait_ge(wt_taken, 1)
                for k in range(CH):
                    for dch in range(CH):
                        last = nc.tensor.transpose(tp[i % 2][:, k * D + dch * P:k * D + (dch + 1) * P],
                                                   w_in[i][:, dch, k * P:(k + 1) * P], ident[:, :])
                last.then_inc(wt_done, 1)
            pe.wait_ge(wt_taken, 3)

            def transposes(source, turned, b, free):
                for k in range(CH):
                    for half in range(NB):
                        u = k * NB + half
                        free(u)
                        for i in range(4):
                            last = nc.tensor.transpose(tp[u % 2][:, i * P:(i + 1) * P],
                                                       source[:, half * 4 + i, k * P:(k + 1) * P], ident[:, :])
                        last.then_inc(turned, 1)

            def natural(lhs, w, done, free):
                for i in range(4):
                    free(i)
                    for t2 in range(2):
                        t = 2 * i + t2
                        for k in range(CH):
                            last = nc.tensor.matmul(pj[i][:, t2 * D:(t2 + 1) * D], lhs[:, k, t * P:(t + 1) * P],
                                                    w[:, k, :], start=(k == 0), stop=(k == CH - 1))
                    last.then_inc(done, 1)

            def attention(b):
                pe.wait_ge(a_loaded, 16 * H * b + 16 * H)
                transposes(a_in, a_turned, b,
                           lambda u: pe.wait_ge(a_copied, 4 * b + u - 1) if u >= 2 else wait(pe, x_copied, 4 * b))
                pe.wait_ge(a_copied, 4 * b + 4)
                natural(aT, wo, wo_done, lambda i: wait(pe, v_taken, 4 * b - 8 + i + 1))

            def batch(b, more=True):
                pe.wait_ge(xn_ready, b + 1)
                transposes(xn, x_turned, b,
                           lambda u: pe.wait_ge(x_copied, 4 * b + u - 1) if u >= 2 else pe.wait_ge(a_copied, 4 * b + 4))
                if more:
                    attention(b + 1)
                pe.wait_ge(mix_ready, 2 * b + 1)
                for g in range(CH):
                    for nh in range(NB):
                        u = g * NB + nh
                        if more:
                            pe.wait_ge(y_taken, 4 * b + 4 + u + 1)
                        elif not isinstance(b, int) or b > 0:
                            pe.wait_ge(v_taken, 4 * b - 4 + u + 1)
                        for k in range(CH):
                            last = nc.tensor.matmul(pj[u][:, :], wT[1][:, k, g * P:(g + 1) * P],
                                                    mix[1][:, k, nh * HALF:(nh + 1) * HALF],
                                                    start=(k == 0), stop=(k == CH - 1))
                        last.then_inc(k_done, 1)
                pe.wait_ge(mix_ready, 2 * b + 2)
                natural(mix[0], wT[0], r_done, lambda i: pe.wait_ge(k_taken, 4 * b + i + 1))
                pe.wait_ge(k_taken, 4 * b + 4)
                natural(kact, wT[2], v_done, lambda i: pe.wait_ge(gate_ready, 4 * b + i + 1))

            attention(0)
            over_batches(pe, batch, ahead=True)


def program(nc, x, Wq, bq, Wk, bk, Wv, bv, Wo, bo, W_r, W_k, W_v, mu_r, mu_k, out):
    qs = nc.dram_tensor("q_parts", [B, CH, GH, PARTS, HD, N], BF16, kind="Internal").ap()
    ks = nc.dram_tensor("k_parts", [B, CH, GH, PARTS, HD, N], BF16, kind="Internal").ap()
    vs = nc.dram_tensor("v_ones", [B, H, P, VROW], F32, kind="Internal").ap()
    att = nc.dram_tensor("att", [B, H, N, HD], F32, kind="Internal").ap()
    project(nc, x, Wq, bq, Wk, bk, Wv, bv, qs, ks, vs)
    attend(nc, qs.rearrange("b c h i d n -> (b c h) i d n"), ks.rearrange("b c h i d n -> (b c h) i d n"),
           vs.rearrange("b h p w -> (b h) p w"), att.rearrange("b h n d -> (b h) n d"))
    finish(nc, x, att, Wo, bo, W_r, W_k, W_v, mu_r, mu_k, out)


_INS = ['L0_attn_x', 'L0_attn_Wq', 'L0_attn_bq', 'L0_attn_Wk', 'L0_attn_bk', 'L0_attn_Wv', 'L0_attn_bv',
        'L0_attn_Wo', 'L0_attn_bo', 'L0_ffn_W_r', 'L0_ffn_W_k', 'L0_ffn_W_v', 'L0_ffn_mu_r', 'L0_ffn_mu_k']


def kernel(**inputs):
    import numpy as _np
    import concourse.bacc as _bacc
    from concourse import mybir as _mybir
    from concourse.bass_utils import run_bass_kernel_spmd as _run

    nc = _bacc.Bacc("TRN2", target_bir_lowering=False, num_devices=1)
    arrays, args = {}, []
    for name in _INS:
        a = _np.ascontiguousarray(inputs[name])
        arrays[f"in_{name}_dram"] = a
        args.append(nc.dram_tensor(f"in_{name}_dram", a.shape, _mybir.dt.from_np(a.dtype), kind="ExternalInput").ap())
    out = nc.dram_tensor("out_dram", (16, 1024, 256), _mybir.dt.float32, kind="ExternalOutput").ap()
    program(nc, *args, out)
    r = _run(nc, [arrays], core_ids=[0])
    return r.results[0]["out_dram"]
```
